# Optimizing a Trainium2 kernel written in Bass

```python
import numpy as np
import jax
import jax.numpy as jnp

def _softmax(x, axis=-1):
    return jax.nn.softmax(x, axis=axis)

def _gelu(x):
    return jax.nn.gelu(x, approximate=True)

def _silu(x):
    return jax.nn.silu(x)

def _sigmoid(x):
    return jax.nn.sigmoid(x)

def _layernorm(x, axis=-1, eps=1e-05):
    m = jnp.mean(x, axis=axis, keepdims=True)
    v = jnp.var(x, axis=axis, keepdims=True)
    return (x - m) / jnp.sqrt(v + eps)

def _scatter_add(tgt, idx, src, axis=0):
    return tgt.at[idx].add(src)

def _segment_sum(src, seg, n):
    return jax.ops.segment_sum(src, seg, n)
kernel_name = 'mk_seq_postln_d1_jaxref_r4_3dbb13'

def setup_inputs(seed: int=0):
    np.random.seed(seed)
    _w = jnp.asarray

    def _L0_attn_setup():
        import jax, jax.numpy as jnp
        import numpy as np
        D_MODEL = 256
        D_STATE = 128
        D_CONV = 4
        EXPAND = 2
        HEADDIM = 64
        CHUNK = 64
        D_INNER = EXPAND * D_MODEL
        NHEADS = D_INNER // HEADDIM
        CONV_DIM = D_INNER + 2 * D_STATE
        D_IN_PROJ = 2 * D_INNER + 2 * D_STATE + NHEADS
        BATCH = 2
        SEQ = 1024
        EPS = 1e-05

        def _segsum(x):
            T = x.shape[-1]
            strict = jnp.tril(jnp.ones((T, T), dtype=bool), k=-1)
            xe = jnp.where(strict, x[..., :, None], 0.0)
            s = jnp.cumsum(xe, axis=-2)
            lower = jnp.tril(jnp.ones((T, T), dtype=bool), k=0)
            return jnp.where(lower, s, -jnp.inf)

        def _ssd(x, A, B, C, chunk):
            b, L, h, p = x.shape
            c = L // chunk
            x = x.reshape(b, c, chunk, h, p)
            A = A.reshape(b, c, chunk, h).transpose(0, 3, 1, 2)
            B = B.reshape(b, c, chunk, -1)
            C = C.reshape(b, c, chunk, -1)
            A_cs = jnp.cumsum(A, axis=-1)
            Lmat = jnp.exp(_segsum(A))
            Y_diag = jnp.einsum('bcln,bcsn,bhcls,bcshp->bclhp', C, B, Lmat, x)
            decay_states = jnp.exp(A_cs[..., -1:] - A_cs)
            states = jnp.einsum('bcln,bhcl,bclhp->bchpn', B, decay_states, x)
            init = jnp.zeros_like(states[:, :1])
            states = jnp.concatenate([init, states], axis=1)
            A_pad = jnp.pad(A_cs[:, :, :, -1], ((0, 0), (0, 0), (1, 0)))
            decay_chunk = jnp.exp(_segsum(A_pad))
            new_states = jnp.einsum('bhzc,bchpn->bzhpn', decay_chunk, states)
            states, final = (new_states[:, :-1], new_states[:, -1])
            Y_off = jnp.einsum('bcln,bchpn,bhcl->bclhp', C, states, jnp.exp(A_cs))
            Y = (Y_diag + Y_off).reshape(b, L, h, p)
            return (Y, final)
        key = jax.random.key(seed)
        ks = jax.random.split(key, 8)
        u = jax.random.normal(ks[0], (BATCH, SEQ, D_MODEL), dtype=jnp.float32)
        in_proj_w = jax.random.normal(ks[1], (D_MODEL, D_IN_PROJ), dtype=jnp.float32) * 0.02
        conv_weight = jax.random.normal(ks[2], (CONV_DIM, 1, D_CONV), dtype=jnp.float32) * 0.02
        conv_bias = jnp.zeros((CONV_DIM,), dtype=jnp.float32)
        dt = jnp.exp(jax.random.uniform(ks[3], (NHEADS,)) * (np.log(0.1) - np.log(0.001)) + np.log(0.001))
        dt = jnp.clip(dt, 0.0001)
        dt_bias = dt + jnp.log(jnp.expm1(dt))
        A_log = jnp.log(jax.random.uniform(ks[4], (NHEADS,), minval=1.0, maxval=16.0))
        D_param = jnp.ones((NHEADS,), dtype=jnp.float32)
        norm_weight = jnp.ones((D_INNER,), dtype=jnp.float32)
        out_proj_w = jax.random.normal(ks[5], (D_INNER, D_MODEL), dtype=jnp.float32) * 0.02
        return dict(u=u, in_proj_w=in_proj_w, conv_weight=conv_weight, conv_bias=conv_bias, dt_bias=dt_bias, A_log=A_log, D_param=D_param, norm_weight=norm_weight, out_proj_w=out_proj_w)
    _L0_attn_in = _L0_attn_setup()

    def _L0_ffn_setup():
        import jax, jax.numpy as jnp
        import numpy as np
        B, S, D, E, F = (2, 512, 256, 8, 1024)
        key = jax.random.key(seed)
        ks = jax.random.split(key, 4)
        return {'hidden_states': jax.random.normal(ks[0], (B, S, D), dtype=jnp.float32), 'Wr': jax.random.normal(ks[1], (D, E), dtype=jnp.float32) * (1.0 / np.sqrt(D)), 'W1': jax.random.normal(ks[2], (E, D, F), dtype=jnp.float32) * (1.0 / np.sqrt(D)), 'b1': jnp.zeros((E, F), dtype=jnp.float32), 'W2': jax.random.normal(ks[3], (E, F, D), dtype=jnp.float32) * (1.0 / np.sqrt(F)), 'b2': jnp.zeros((E, D), dtype=jnp.float32)}
    _L0_ffn_in = _L0_ffn_setup()
    _d = {'L0_attn_u': _L0_attn_in['u'], 'L0_attn_in_proj_w': _L0_attn_in['in_proj_w'], 'L0_attn_conv_weight': _L0_attn_in['conv_weight'], 'L0_attn_conv_bias': _L0_attn_in['conv_bias'], 'L0_attn_dt_bias': _L0_attn_in['dt_bias'], 'L0_attn_A_log': _L0_attn_in['A_log'], 'L0_attn_D_param': _L0_attn_in['D_param'], 'L0_attn_norm_weight': _L0_attn_in['norm_weight'], 'L0_attn_out_proj_w': _L0_attn_in['out_proj_w'], 'L0_ffn_Wr': _L0_ffn_in['Wr'], 'L0_ffn_W1': _L0_ffn_in['W1'], 'L0_ffn_b1': _L0_ffn_in['b1'], 'L0_ffn_W2': _L0_ffn_in['W2'], 'L0_ffn_b2': _L0_ffn_in['b2']}
    _x0 = _d['L0_attn_u']
    _d['L0_attn_u'] = jax.random.normal(jax.random.fold_in(jax.random.key(seed), 1), (2, 2048, 256), dtype=_x0.dtype)
    del _x0
    return _d

def reference(L0_attn_u, L0_attn_in_proj_w, L0_attn_conv_weight, L0_attn_conv_bias, L0_attn_dt_bias, L0_attn_A_log, L0_attn_D_param, L0_attn_norm_weight, L0_attn_out_proj_w, L0_ffn_Wr, L0_ffn_W1, L0_ffn_b1, L0_ffn_W2, L0_ffn_b2):

    def _L0_attn_ref(u, in_proj_w, conv_weight, conv_bias, dt_bias, A_log, D_param, norm_weight, out_proj_w):
        import jax, jax.numpy as jnp
        import numpy as np
        D_MODEL = 256
        D_STATE = 128
        D_CONV = 4
        EXPAND = 2
        HEADDIM = 64
        CHUNK = 64
        D_INNER = EXPAND * D_MODEL
        NHEADS = D_INNER // HEADDIM
        CONV_DIM = D_INNER + 2 * D_STATE
        D_IN_PROJ = 2 * D_INNER + 2 * D_STATE + NHEADS
        BATCH = 2
        SEQ = 1024
        EPS = 1e-05

        def _segsum(x):
            T = x.shape[-1]
            strict = jnp.tril(jnp.ones((T, T), dtype=bool), k=-1)
            xe = jnp.where(strict, x[..., :, None], 0.0)
            s = jnp.cumsum(xe, axis=-2)
            lower = jnp.tril(jnp.ones((T, T), dtype=bool), k=0)
            return jnp.where(lower, s, -jnp.inf)

        def _ssd(x, A, B, C, chunk):
            b, L, h, p = x.shape
            c = L // chunk
            x = x.reshape(b, c, chunk, h, p)
            A = A.reshape(b, c, chunk, h).transpose(0, 3, 1, 2)
            B = B.reshape(b, c, chunk, -1)
            C = C.reshape(b, c, chunk, -1)
            A_cs = jnp.cumsum(A, axis=-1)
            Lmat = jnp.exp(_segsum(A))
            Y_diag = jnp.einsum('bcln,bcsn,bhcls,bcshp->bclhp', C, B, Lmat, x)
            decay_states = jnp.exp(A_cs[..., -1:] - A_cs)
            states = jnp.einsum('bcln,bhcl,bclhp->bchpn', B, decay_states, x)
            init = jnp.zeros_like(states[:, :1])
            states = jnp.concatenate([init, states], axis=1)
            A_pad = jnp.pad(A_cs[:, :, :, -1], ((0, 0), (0, 0), (1, 0)))
            decay_chunk = jnp.exp(_segsum(A_pad))
            new_states = jnp.einsum('bhzc,bchpn->bzhpn', decay_chunk, states)
            states, final = (new_states[:, :-1], new_states[:, -1])
            Y_off = jnp.einsum('bcln,bchpn,bhcl->bclhp', C, states, jnp.exp(A_cs))
            Y = (Y_diag + Y_off).reshape(b, L, h, p)
            return (Y, final)
        b, L, _ = u.shape
        zxbcdt = u @ in_proj_w
        z = zxbcdt[..., :D_INNER]
        xBC = zxbcdt[..., D_INNER:D_INNER + CONV_DIM]
        dt = jax.nn.softplus(zxbcdt[..., -NHEADS:] + dt_bias)
        cw = jnp.squeeze(conv_weight, axis=1).T
        xp = jnp.pad(xBC, ((0, 0), (D_CONV - 1, 0), (0, 0)))
        conv = sum((xp[:, i:i + L, :] * cw[i] for i in range(D_CONV))) + conv_bias
        xBC = conv * jax.nn.sigmoid(conv)
        x = xBC[..., :D_INNER].reshape(b, L, NHEADS, HEADDIM)
        Bm = xBC[..., D_INNER:D_INNER + D_STATE]
        Cm = xBC[..., D_INNER + D_STATE:]
        A = -jnp.exp(A_log)
        y, _ = _ssd(x * dt[..., None], A[None, None, :] * dt, Bm, Cm, CHUNK)
        y = y + D_param[None, None, :, None] * x
        y = y.reshape(b, L, D_INNER)
        y = y * (z * jax.nn.sigmoid(z))
        y = y * jax.lax.rsqrt(jnp.mean(jnp.square(y), axis=-1, keepdims=True) + EPS) * norm_weight
        return y @ out_proj_w

    def _L0_ffn_ref(hidden_states, Wr, W1, b1, W2, b2):
        import jax, jax.numpy as jnp
        import numpy as np
        B, S, D, E, F = (2, 512, 256, 8, 1024)
        b, s, d = hidden_states.shape
        e = Wr.shape[1]
        x = hidden_states.reshape(b * s, d)
        router_logits = x @ Wr
        router_probs = jax.nn.softmax(router_logits, axis=-1)
        expert_idx = jnp.argmax(router_probs, axis=-1)
        p_max = jnp.max(router_probs, axis=-1, keepdims=True)

        def expert_mlp(w1, bb1, w2, bb2):
            h = jax.nn.gelu(x @ w1 + bb1, approximate=False)
            return h @ w2 + bb2
        outs = jax.vmap(expert_mlp)(W1, b1, W2, b2)
        onehot = jax.nn.one_hot(expert_idx, e, dtype=x.dtype)
        next_states = jnp.einsum('te,etd->td', onehot, outs)
        out = p_max * next_states
        return out.reshape(b, s, d)
    x = L0_attn_u
    x = _layernorm(x + _L0_attn_ref(x, L0_attn_in_proj_w, L0_attn_conv_weight, L0_attn_conv_bias, L0_attn_dt_bias, L0_attn_A_log, L0_attn_D_param, L0_attn_norm_weight, L0_attn_out_proj_w), axis=-1)
    x = _layernorm(x + _L0_ffn_ref(x, L0_ffn_Wr, L0_ffn_W1, L0_ffn_b1, L0_ffn_W2, L0_ffn_b2), axis=-1)
    return x

_drawn_inputs = setup_inputs


def setup_inputs(seed=0):
    import zlib

    import numpy as np

    out = dict(_drawn_inputs(seed))
    spreads = {'L0_attn_conv_bias': (0.0, 0.1),
     'L0_attn_D_param': (1.0, 0.2),
     'L0_attn_norm_weight': (1.0, 0.2),
     'L0_ffn_b1': (0.0, 0.313),
     'L0_ffn_b2': (0.0, 0.1)}
    factors = {'L0_attn_dt_bias': 8.0, 'L0_attn_A_log': 8.0}
    for name, (base, spread) in spreads.items():
        noise = np.random.default_rng([zlib.crc32(name.encode()), seed]).standard_normal(out[name].shape)
        drawn = base * np.exp(spread * noise) if base else spread * noise
        out[name] = jnp.asarray(drawn.astype(out[name].dtype))
    for name, factor in factors.items():
        out[name] = (out[name] * factor).astype(out[name].dtype)
    return out
```

```python
from contextlib import ExitStack

import numpy as np

import concourse.bass as bass
from concourse import mybir

ALU = mybir.AluOpType
ACT = mybir.ActivationFunctionType
AX = mybir.AxisListType.X
F32 = mybir.dt.float32
I32 = mybir.dt.int32

P = 128
NB, L, D = 2, 2048, 256
DI, NS, NH, HD = 512, 128, 8, 64
TAPS = 4
NPROJ = 2 * DI + 2 * NS + NH
XT_TILES = (DI + 2 * NS) // P
XD_TILES = DI // P
NE, FF = 8, 1024
EPS = 1e-5
T = NB * L
NC = T // P
BLOCKS = T // P + NE
LATE = 3
KD, KF, KI = D // P, FF // P, DI // P

M_ID, M_LE, M_GT, M_LT = range(4)
N_MASKS = 4
CW = N_MASKS * P + BLOCKS + NE + NC + P
FILLS = 7
SP_STEPS = 20
ROUTE_ONEHOT = 8


def constants():
    k, m = np.arange(P)[:, None], np.arange(P)[None, :]
    masks = [k == m, k <= m, k > m, k < m]
    c, rest = np.zeros((P, CW), np.float32), N_MASKS * P
    for n, mask in enumerate(masks):
        c[:, n * P:(n + 1) * P] = mask
    c[:, rest:rest + BLOCKS] = np.arange(BLOCKS)
    c[:, rest + BLOCKS:rest + BLOCKS + NE] = NE - np.arange(NE)
    chunk = np.arange(NC)
    c[:, rest + BLOCKS + NE:CW - P] = (chunk % NB) * L + (chunk // NB) * P + k + 1
    c[:, CW - P:] = np.arange(P)
    return c


def wait(eng, sem, n):
    if not isinstance(n, int) or n > 0:
        eng.wait_ge(sem, n)


def settled(eng, turns):
    eng.sem_inc(turns, 1)


def edge(eng, sem, c, n):
    if isinstance(c, int):
        wait(eng, sem, n)


def on(c):
    return not isinstance(c, int) or 0 <= c < NC


def mamba_steps(eng, step, first):
    peeled, lag = 6, 4
    for t in range(first, peeled):
        step(t, t % 2)
    with eng.Fori(peeled // 2, NC // 2 - 1) as j:
        for par in range(2):
            step(2 * j + par, par)
    for t in range(NC - 2, NC + lag):
        step(t, t % 2)


def pre_steps(eng, pair_step):
    for pair in range(4):
        pair_step(pair, pair)
    with eng.Fori(1, NC // 8) as q:
        for r in range(4):
            pair_step(4 * q + r, r)


def block_steps(eng, step, first, last, before=None):
    for i in range(first, 8):
        step(i, i % 4, None)
    with eng.Fori(2, BLOCKS // 4 - 1) as j:
        held = before(j) if before else None
        for r in range(4):
            step(4 * j + r, r, held)
    for i in range(BLOCKS - 4, last):
        step(i, i % 4, None)


def build(nc, u, in_proj_w, conv_w, conv_b, dt_bias, a_log, d_param, norm_w, out_proj_w,
          wr, w1, b1, w2, b2, consts, out):
    x1_rows = nc.dram_tensor("x1_rows", [T + 1, D], F32, kind="Internal").ap()
    ctx = ExitStack()
    with ctx:
        wsize = KD * FF + KF * D
        wtotal = NE * wsize
        arena = ctx.enter_context(nc.sbuf_tensor("arena", [P, 53100], F32))
        at = [0]

        def carve(*shape):
            n = int(np.prod(shape))
            v = arena[:, at[0]:at[0] + n]
            at[0] += n
            if len(shape) == 2:
                v = v.rearrange("p (a b) -> p a b", a=shape[0])
            elif len(shape) == 3:
                v = v.rearrange("p (a b c) -> p a b c", a=shape[0], b=shape[1])
            return v

        w1_sb = arena[:, 0:NE * KD * FF].rearrange("p (e k f) -> p e k f", e=NE, k=KD)
        w2_sb = arena[:, NE * KD * FF:wtotal].rearrange("p (e k d) -> p e k d", e=NE, k=KF)
        at[0] = wtotal
        cst = carve(CW)
        masks = cst[:, 0:N_MASKS * P].rearrange("p (n m) -> p n m", n=N_MASKS)
        ident = masks[:, M_ID, :]
        iota_blk = cst[:, N_MASKS * P:N_MASKS * P + BLOCKS]
        prio = cst[:, N_MASKS * P + BLOCKS:N_MASKS * P + BLOCKS + NE]
        ids1 = cst[:, N_MASKS * P + BLOCKS + NE:CW - P]
        iota_slot = cst[:, CW - P:CW]
        ones = carve(P)
        half_neg = carve(2)
        logits = carve(NC, NE)
        wr_sb = carve(KD, NE)
        zrow = carve(D)
        persistent_end = at[0]

        b1_rep = carve(NE, FF)
        b2_rep = carve(NE, D)
        idx_f = carve(BLOCKS)
        idx_z = carve(BLOCKS)
        idx_i = carve(BLOCKS).bitcast(I32)
        prob_blk = carve(BLOCKS)
        eb_f = carve(BLOCKS)
        eb_i = carve(BLOCKS).bitcast(I32)
        idx_col = [carve(1).bitcast(I32) for _ in range(4)]
        idx_out = [carve(1).bitcast(I32) for _ in range(4)]
        temp_start = at[0]
        xg = [carve(D) for _ in range(4)]
        yo = [carve(D) for _ in range(4)]
        xgT = [carve(KD, P) for _ in range(2)]
        hp = [carve(FF) for _ in range(2)]
        h_sb = [carve(FF) for _ in range(2)]
        hT = carve(KF, P)
        st2 = [carve(6) for _ in range(2)]
        mv2 = [carve(2) for _ in range(2)]
        rstd2 = [carve(2) for _ in range(2)]
        assert at[0] <= 53100
        at[0] = temp_start
        lt = carve(NC, NE)
        ex = carve(NC, NE)
        onehot = carve(NC, NE)
        pref = [carve(NC, NE) for _ in range(2)]
        small = carve(16, NC)
        GT = 4
        oh_slot = carve(GT, P)
        oh_blk = carve(2, GT, BLOCKS)
        ge = carve(BLOCKS, NE)
        tiny = carve(16, NE)
        assert at[0] <= 53100, at[0]

        at[0] = persistent_end
        w_in = carve(KD, NPROJ)
        w_out = carve(KI, D)
        nw_col = carve(KI)
        cw_sb = carve(XT_TILES, TAPS)
        cb_sb = carve(XT_TILES)
        d_row = carve(NH)
        dtb_row = carve(NH)
        negA = carve(NH)
        a_all = carve(NC, NH)
        dt_all = carve(NC, NH)
        e_all = carve(NC, NH)
        cd_all = carve(NC, NH)
        dd_all = carve(NC, NH)
        u_in = [carve(D) for _ in range(2)]
        uT = [carve(KD, P) for _ in range(2)]
        u_res = [carve(D) for _ in range(2)]
        xs = [carve(XT_TILES, P) for _ in range(2)]
        zs = [carve(DI) for _ in range(2)]
        xdt = [carve(NH, HD) for _ in range(2)]
        state = [carve(NH, HD) for _ in range(2)]
        y = [carve(NH, HD) for _ in range(2)]
        yT = carve(KI, P)
        x1T = carve(KD, P)
        cbm = [carve(P) for _ in range(2)]
        b_sb = [carve(P) for _ in range(2)]
        ssq = carve(2)
        rms = carve(2)
        bst = [carve(6) for _ in range(2)]
        mv = [carve(2) for _ in range(2)]
        rstd = carve(2)
        assert at[0] <= 53100, at[0]
        at[0] = NE * KD * FF + (NE - LATE) * KF * D
        xbc = [carve(XT_TILES, TAPS - 1 + P) for _ in range(2)]
        cv = [carve(XT_TILES, P) for _ in range(2)]
        x_sb = [carve(NH, HD) for _ in range(2)]
        xdd = [carve(NH, HD) for _ in range(2)]
        assert at[0] <= wtotal, (at[0], wtotal)
        at[0] = (NE - LATE) * KD * FF
        ub = [carve(NH, P) for _ in range(2)]
        em = [carve(NH, P) for _ in range(2)]
        junk = carve(DI)
        xD = [carve(NH, HD) for _ in range(2)]
        assert at[0] <= NE * KD * FF
        at[0] = (NE - LATE) * KD * FF
        pre_u = [carve(NB, D) for _ in range(4)]
        pre_uT = [carve(NB * KD, P) for _ in range(2)]
        dtx = carve(NC, NH)
        dta = carve(NC, NH)
        dts = carve(NC, NH)
        dtq = carve(NC, NH)
        dtp = carve(NC, NH)
        assert at[0] <= NE * KD * FF

        bank = [ctx.enter_context(nc.psum_tensor(f"bank{n}", [P, 512], F32)) for n in range(8)]

        def sem(name):
            return ctx.enter_context(nc.semaphore(name))

        s_const = sem("const_loaded")
        s_param = sem("dt_params_loaded")
        s_param2 = sem("mamba_params_loaded")
        s_early = sem("early_experts_loaded")
        s_late = sem("late_experts_loaded")
        s_zrow = sem("zero_row_stored")
        s_fill = sem("fills_done")
        s_pool_turns, s_dve_turns = sem("pool_turns"), sem("dve_turns")
        s_wout = sem("out_proj_scaled")
        s_pre_u = [sem(f"pre_u_loaded{n}") for n in range(4)]
        s_pre_t = sem("pre_transposed")
        s_pre_ev = sem("pre_uT_ready")
        s_pre_dt = sem("pre_dt_product")
        s_negA = sem("negA_steps")
        s_sp = sem("softplus_steps")
        s_spx = sem("softplus_exp")
        s_sums = sem("chunk_sums")
        s_sumx = sem("chunk_sums_exp")
        s_pre = sem("dt_phase_done")
        s_uin = [sem(f"u_in_loaded{n}") for n in range(2)]
        s_ures = [sem(f"u_res_loaded{n}") for n in range(2)]
        s_x1st = [sem(f"x1_stored{n}") for n in range(2)]
        q_ut, q_ute = sem("u_transposed"), sem("uT_ready")
        q_inx, q_xbe, q_halo = sem("xbc_product"), sem("xbc_ready"), sem("halo_copied")
        q_conv, q_silx = sem("conv_steps"), sem("xs_ready")
        q_inz, q_silz = sem("z_product"), sem("zs_ready")
        q_xt, q_xte = sem("x_transposed"), sem("x_ready")
        q_bc, q_be, q_cbm = sem("b_and_cb"), sem("b_ready"), sem("cb_masked")
        q_ub, q_seg, q_exp, q_m = sem("a_mask_ready"), sem("segment_sums"), sem("decay_ready"), sem("m_ready")
        q_xdt, q_xdd, q_xd = sem("xdt_ready"), sem("xdd_ready"), sem("xD_ready")
        q_y, q_yv, q_sq = sem("y_products"), sem("y_steps"), sem("y_squared")
        q_st, q_s = sem("state_product"), sem("state_updated")
        q_rms, q_yt, q_yte = sem("rms_steps"), sem("y_transposed"), sem("yT_ready")
        q_op, q_r, q_rstd, q_x1 = sem("out_product"), sem("residual_steps"), sem("rstd_steps"), sem("x1_ready")
        q_rt, q_rte, q_lg, q_lge = sem("x1_transposed"), sem("x1T_ready"), sem("logit_product"), sem("logits_ready")
        s_rv, s_rx, s_rp, s_ohs, s_inv = (sem("route_steps"), sem("route_exp"), sem("route_products"),
                                          sem("onehots_ready"), sem("slots_product"))
        s_route = sem("routing_done")
        g_idx, g_x = sem("gather_index_ready"), [sem(f"rows_gathered{n}") for n in range(4)]
        g_xt, g_xte = sem("xg_transposed"), sem("xgT_ready")
        g_w1, g_hb, g_h = sem("w1_product"), sem("h_biased"), sem("h_ready")
        g_ht, g_hte, g_w2 = sem("h_transposed"), sem("hT_ready"), sem("w2_product")
        g_r, g_rs, g_y = sem("block_residual_steps"), sem("block_rstd_steps"), sem("block_rows_ready")
        g_oidx, g_out = sem("scatter_index_ready"), [sem(f"rows_scattered{n}") for n in range(4)]

        def chunk_rows(c, par):
            return (c - par) * (P // 2) + par * L

        block = ctx.enter_context(nc.Block())

        @block.sync
        def _(sp):
            sp.dma_start(w_in[:, :, :], in_proj_w.rearrange("(k p) n -> p k n", p=P)).then_inc(s_param, 16)
            sp.dma_start(cst, consts).then_inc(s_const, 16)
            sp.dma_start(dtb_row, dt_bias.partition_broadcast(P)).then_inc(s_param, 16)
            sp.dma_start(negA, a_log.partition_broadcast(P)).then_inc(s_param, 16)
            def load_pair(pair, r):
                wait(sp, s_pre_t, pair - 3)
                sp.dma_start(pre_u[r], u[:, bass.ds(pair * P, P), :].rearrange("b p d -> p b d")).then_inc(s_pre_u[r], 16)

            pre_steps(sp, load_pair)
            sp.dma_start(w_out[:, :, :], out_proj_w.rearrange("(k p) n -> p k n", p=P)).then_inc(s_param2, 16)
            sp.dma_start(nw_col, norm_w).then_inc(s_param2, 16)
            sp.dma_start(cw_sb[:, :, :], conv_w).then_inc(s_param2, 16)
            sp.dma_start(cb_sb, conv_b).then_inc(s_param2, 16)
            sp.dma_start(d_row, d_param.partition_broadcast(P)).then_inc(s_param2, 16)
            sp.dma_start(wr_sb[:, :, :], wr.rearrange("(k p) e -> p k e", p=P)).then_inc(s_param2, 16)
            sp.wait_ge(s_fill, 1)
            sp.dma_start(x1_rows[T:T + 1, :], zrow[0:1, :]).then_inc(s_zrow, 16)

            def step(t, par):
                if on(t - 4):
                    wait(sp, q_x1, t - 3)
                    sp.dma_start(x1_rows[bass.ds(chunk_rows(t - 4, par), P), :], u_res[par]
                                 ).then_inc(s_x1st[par], 16)
                if on(t + 2):
                    wait(sp, q_ut, t + 1)
                    c = t + 2
                    sp.dma_start(u_in[par], u[par, bass.ds((c - par) * (P // 2), P), :]).then_inc(s_uin[par], 16)
                if on(t - 2):
                    wait(sp, s_x1st[par], 8 * (t - 4 - par) + 16)
                    wait(sp, q_rt, t - 3)
                    sp.dma_start(u_res[par], u[par, bass.ds((t - 2 - par) * (P // 2), P), :]
                                 ).then_inc(s_ures[par], 16)

            mamba_steps(sp, step, -2)

            sp.wait_ge(q_lge, NC)
            sp.wait_ge(q_s, NC * 8)
            sp.wait_ge(q_x1, NC)
            sp.wait_ge(q_sq, NC)
            for e in range(NE - LATE, NE):
                sp.dma_start(w1_sb[:, e, :, :], w1[e].rearrange("(k p) f -> p k f", p=P)).then_inc(s_late, 16)
                sp.dma_start(w2_sb[:, e, :, :], w2[e].rearrange("(k p) d -> p k d", p=P)).then_inc(s_late, 16)
            sp.dma_start(b1_rep[:, :, :].rearrange("p e f -> p (e f)"),
                         b1.rearrange("e f -> (e f)").partition_broadcast(P)).then_inc(s_late, 16)
            sp.dma_start(b2_rep[:, :, :].rearrange("p e f -> p (e f)"),
                         b2.rearrange("e f -> (e f)").partition_broadcast(P)).then_inc(s_late, 16)

        @block.gpsimd
        def _(pool):
            pool.memset(zrow, 0.0).then_inc(s_fill, 1)
            pool.memset(ones, 1.0).then_inc(s_fill, 1)
            pool.memset(half_neg, -0.5).then_inc(s_fill, 1)
            pool.memset(state[0][:, :, :], 0.0).then_inc(s_fill, 1)
            pool.memset(state[1][:, :, :], 0.0).then_inc(s_fill, 1)
            for par in range(2):
                pool.memset(xbc[par][:, :, 0:TAPS - 1], 0.0).then_inc(s_fill, 1)
            pool.wait_ge(s_fill, FILLS)
            pool.wait_ge(s_param2, 96)
            pool.wait_ge(s_pre, 1)

            def step(t, par):
                c, p = t - 1, 1 - par
                if on(c):
                    wait(pool, q_xte, c + 1)
                    wait(pool, q_st, c - 1)
                    pool.tensor_tensor(xdd[p], x_sb[p], dd_all[:, bass.ds(c, 1), :].rearrange("p o h -> p (o h)")
                                       .unsqueeze(2).broadcast_to([P, NH, HD]), ALU.mult).then_inc(q_xdd, 1)
                    wait(pool, q_yv, 4 * (c - 1))
                    pool.tensor_tensor(xD[p], x_sb[p], d_row.unsqueeze(2).broadcast_to([P, NH, HD]),
                                       ALU.mult).then_inc(q_xd, 1)
                c, p = t - 2, par
                if on(c):
                    wait(pool, q_sq, c + 1)
                    wait(pool, q_r, 3 * (c - 2) + 1)
                    settled(pool, s_pool_turns)
                    pool.tensor_scalar(rms[:, p:p + 1], ssq[:, p:p + 1], 1.0 / DI, EPS, ALU.mult, ALU.add
                                       ).then_inc(q_rms, 1)
                    wait(pool, q_rms, 2 * c + 1)
                    pool.tensor_tensor(rms[:, p:p + 1], rms[:, p:p + 1], half_neg[:, 0:1], ALU.pow).then_inc(q_rms, 1)
                c, p = t - 3, 1 - par
                if on(c):
                    wait(pool, q_r, 3 * c + 3)
                    wait(pool, q_x1, c - 1)
                    settled(pool, s_pool_turns)
                    pool.tensor_scalar(rstd[:, p:p + 1], mv[p][:, 1:2], EPS, None, ALU.add).then_inc(q_rstd, 1)
                    wait(pool, q_rstd, 2 * c + 1)
                    pool.tensor_tensor(rstd[:, p:p + 1], rstd[:, p:p + 1], half_neg[:, 0:1], ALU.pow
                                       ).then_inc(q_rstd, 1)

            mamba_steps(pool, step, 1)

            pool.wait_ge(s_route, 1)
            pool.wait_ge(s_zrow, 16)
            for par in range(2):
                pool.wait_ge(s_x1st[par], 16 * NC // 2)
            limit_in, limit_out = T, T - 1

            def bstep(i, r, held):
                ok = lambda k: not isinstance(k, int) or 0 <= k < BLOCKS
                if ok(i + 2):
                    c, q = i + 2, (r + 2) % 4
                    wait(pool, g_y, c - 3)
                    pool.tensor_copy(idx_col[q], idx_i[:, bass.ds(c, 1)]).then_inc(g_idx, 1)
                    wait(pool, g_idx, c + 1)
                    settled(pool, s_pool_turns)
                    pool.indirect_dma_start(xg[q], None, x1_rows[:, :],
                                            bass.IndirectOffsetOnAxis(ap=idx_col[q], axis=0),
                                            bounds_check=limit_in, oob_is_err=False).then_inc(g_x[q], 16)
                if ok(i - 1):
                    c, q = i - 1, (r - 1) % 4
                    p = (r - 1) % 2
                    wait(pool, g_r, 4 * c + 4)
                    wait(pool, g_y, c - 1)
                    settled(pool, s_pool_turns)
                    pool.tensor_scalar(rstd2[p][:, 0:1], mv2[p][:, 1:2], EPS, None, ALU.add).then_inc(g_rs, 1)
                    wait(pool, g_rs, 2 * c + 1)
                    pool.tensor_tensor(rstd2[p][:, 1:2], rstd2[p][:, 0:1], half_neg[:, 0:1], ALU.pow
                                       ).then_inc(g_rs, 1)
                if ok(i - 2):
                    c, q = i - 2, (r - 2) % 4
                    wait(pool, g_out[q], 4 * (c - q))
                    pool.tensor_copy(idx_out[q], idx_i[:, bass.ds(c, 1)]).then_inc(g_oidx, 1)
                    wait(pool, g_oidx, c + 1)
                    wait(pool, g_y, c + 1)
                    settled(pool, s_pool_turns)
                    pool.indirect_dma_start(out, bass.IndirectOffsetOnAxis(ap=idx_out[q], axis=0), yo[q], None,
                                            bounds_check=limit_out, oob_is_err=False).then_inc(g_out[q], 16)

            block_steps(pool, bstep, -2, BLOCKS + 2)
            for q in range(4):
                pool.wait_ge(g_out[q], 16 * BLOCKS // 4)

        @block.tensor
        def _(pe):
            pe.wait_ge(s_const, 16)
            pe.wait_ge(s_param, 48)
            def pre_pair(pair, r):
                p = r % 2
                pe.wait_ge(s_pre_u[r], 4 * (pair - r) + 16)
                wait(pe, s_pre_ev, pair - 1)
                for b in range(NB):
                    for k in range(KD):
                        mm = pe.transpose(bank[p][:, (b * KD + k) * P:(b * KD + k + 1) * P],
                                          pre_u[r][:, b, k * P:(k + 1) * P], ident)
                mm.then_inc(s_pre_t, 1)
                pe.wait_ge(s_pre_ev, pair + 1)
                for b in range(NB):
                    for k in range(KD):
                        mm = pe.matmul(bank[2][:, bass.ds(pair * (NB * NH) + b * NH, NH)],
                                       pre_uT[p][:, b * KD + k, :], w_in[:, k, NPROJ - NH:NPROJ],
                                       start=(k == 0), stop=(k == KD - 1))
                mm.then_inc(s_pre_dt, 1)

            pre_steps(pe, pre_pair)
            pe.wait_ge(s_sp, SP_STEPS)
            flat = lambda v: v.rearrange("p c h -> p (c h)")
            pe.wait_ge(s_fill, FILLS)
            pe.matmul(bank[3][:, 0:NC * NH], masks[:, M_LE, :], flat(a_all), start=True, stop=True)
            pe.matmul(bank[4][:, 0:NC * NH], masks[:, M_GT, :], flat(a_all), start=True, stop=True)
            pe.matmul(bank[5][:, 0:NC * NH], ones, flat(a_all), start=True, stop=True).then_inc(s_sums, 1)
            pe.wait_ge(s_pre, 1)
            pe.wait_ge(s_sumx, 3)
            pe.wait_ge(s_param2, 96)
            pe.wait_ge(s_wout, 1)

            def step(t, par):
                c, p = t - 3, 1 - par
                if on(c):
                    wait(pe, q_yv, 4 * c + 4)
                    wait(pe, q_silz, min(c + 2, NC) if isinstance(c, int) else c + 2)
                    edge(pe, q_yte, c, c)
                    yf = y[p].rearrange("p h d -> p (h d)")
                    for k in range(KI):
                        mm = pe.transpose(bank[2][:, k * P:(k + 1) * P], yf[:, k * P:(k + 1) * P], ident)
                    mm.then_inc(q_yt, 1)
                c, p = t, par
                if on(c):
                    wait(pe, q_ute, c + 1)
                    wait(pe, q_yv, 4 * (c - 3) + 2)
                    edge(pe, q_xbe, c, 2 * c)
                    for m in range(XT_TILES):
                        lo = DI + m * P
                        for k in range(KD):
                            mm = pe.matmul(bank[m // 3][:, (m % 3) * P:(m % 3 + 1) * P], w_in[:, k, lo:lo + P],
                                           uT[p][:, k, :], start=(k == 0), stop=(k == KD - 1))
                    mm.then_inc(q_inx, 1)
                c, p = t - 3, 1 - par
                if on(c):
                    wait(pe, q_yte, c + 1)
                    wait(pe, q_rte, c - 1)
                    edge(pe, q_r, c, 3 * (c - 1) + 1)
                    for k in range(KI):
                        mm = pe.matmul(bank[3][:, 0:D], yT[:, k, :], w_out[:, k, :], start=(k == 0), stop=(k == KI - 1))
                    mm.then_inc(q_op, 1)
                c, p = t - 1, 1 - par
                if on(c):
                    wait(pe, q_silx, c + 1)
                    wait(pe, q_s, 8 * (c - 1))
                    edge(pe, q_xte, c, c)
                    for m in range(XD_TILES):
                        mm = pe.transpose(bank[4][:, m * P:(m + 1) * P], xs[p][:, m, :], ident)
                    mm.then_inc(q_xt, 1)
                    wait(pe, q_lge, c - 3)
                    edge(pe, q_be, c, c)
                    edge(pe, q_cbm, c, c)
                    pe.transpose(bank[7][:, 0:P], xs[p][:, XD_TILES, :], ident)
                    pe.matmul(bank[7][:, P:2 * P], xs[p][:, XD_TILES, :], xs[p][:, XD_TILES + 1, :],
                              start=True, stop=True).then_inc(q_bc, 1)
                    wait(pe, q_ub, c + 1)
                    wait(pe, q_ute, min(c + 2, NC) if isinstance(c, int) else c + 2)
                    wait(pe, q_exp, c)
                    for n in range(2):
                        mm = pe.matmul(bank[5 + n][:, :], masks[:, M_GT, :],
                                       ub[p][:, 4 * n:4 * n + 4, :].rearrange("p h l -> p (h l)"), start=True, stop=True)
                    mm.then_inc(q_seg, 1)
                    wait(pe, q_yte, c - 1)
                    edge(pe, q_silz, c, c)
                    for k in range(KD):
                        mm = pe.matmul(bank[2][:, :], uT[p][:, k, :], w_in[:, k, 0:DI], start=(k == 0), stop=(k == KD - 1))
                    mm.then_inc(q_inz, 1)
                c, p = t - 2, par
                if on(c):
                    wait(pe, q_m, c + 1)
                    wait(pe, q_xdt, c + 1)
                    wait(pe, q_xbe, min(2 * (c + 3), 2 * NC) if isinstance(c, int) else 2 * (c + 3))
                    edge(pe, q_yv, c, 4 * (c - 1) + 2)
                    for h in range(NH):
                        pe.matmul(bank[0][:, h * HD:(h + 1) * HD], em[p][:, h, :], xdt[p][:, h, :], start=True, stop=True)
                    wait(pe, q_s, 8 * (c - 1))
                    pe.matmul(bank[1][:, :], xs[p][:, XD_TILES + 1, :], state[p].rearrange("p h d -> p (h d)"),
                              start=True, stop=True).then_inc(q_y, 1)
                c, p = t - 4, par
                if on(c):
                    wait(pe, q_x1, c + 1)
                    wait(pe, q_r, min(3 * (c + 1) + 1, 3 * NC) if isinstance(c, int) else 3 * (c + 1) + 1)
                    edge(pe, q_rte, c, c)
                    for k in range(KD):
                        mm = pe.transpose(bank[3][:, k * P:(k + 1) * P], u_res[p][:, k * P:(k + 1) * P], ident)
                    mm.then_inc(q_rt, 1)
                c, p = t - 2, par
                if on(c):
                    wait(pe, q_xdd, c + 1)
                    wait(pe, q_be, c + 1)
                    wait(pe, q_xte, min(c + 2, NC) if isinstance(c, int) else c + 2)
                    edge(pe, q_s, c, 8 * c)
                    pe.matmul(bank[4][:, :], b_sb[p], xdd[p].rearrange("p h d -> p (h d)"),
                              start=True, stop=True).then_inc(q_st, 1)
                c, p = t - 4, par
                if on(c):
                    wait(pe, q_rte, c + 1)
                    wait(pe, q_be, min(c + 4, NC) if isinstance(c, int) else c + 4)
                    wait(pe, q_cbm, min(c + 4, NC) if isinstance(c, int) else c + 4)
                    edge(pe, q_lge, c, c)
                    for k in range(KD):
                        mm = pe.matmul(bank[7][:, 0:NE], x1T[:, k, :], wr_sb[:, k, :], start=(k == 0), stop=(k == KD - 1))
                    mm.then_inc(q_lg, 1)
                c, p = t + 1, 1 - par
                if on(c):
                    wait(pe, s_uin[p], 8 * (c - p) + 16)
                    wait(pe, q_exp, c - 1)
                    edge(pe, q_ute, c, c)
                    for k in range(KD):
                        mm = pe.transpose(bank[5][:, k * P:(k + 1) * P], u_in[p][:, k * P:(k + 1) * P], ident)
                    mm.then_inc(q_ut, 1)

            mamba_steps(pe, step, -1)

            pe.wait_ge(s_rv, ROUTE_ONEHOT)
            pe.wait_ge(q_lge, NC)
            pe.matmul(bank[0][:, 0:NC * NE], masks[:, M_LT, :], flat(onehot), start=True, stop=True)
            pe.matmul(bank[1][:, 0:NC * NE], ones, flat(onehot), start=True, stop=True).then_inc(s_rp, 1)
            for c in range(NC):
                if c % GT == 0:
                    pe.wait_ge(s_ohs, 3 * (c // GT + 1))
                mm = pe.matmul(bank[2][:, 0:2 * BLOCKS], oh_slot[:, c % GT, :], oh_blk[:, :, c % GT, :],
                               start=(c == 0), stop=(c == NC - 1))
                if c % GT == GT - 1:
                    mm.then_inc(s_inv, 1)

            pe.wait_ge(s_route, 1)
            pe.wait_ge(s_early, 32 * (NE - LATE))
            pe.wait_ge(s_late, 32 * LATE + 32)

            def experts(j):
                return [pe.value_load(eb_i[0:1, bass.ds(4 * j + r, 1)], min_val=0, max_val=NE - 1)
                        for r in range(-1, 4)]

            def bstep(i, r, held):
                ok = lambda k: not isinstance(k, int) or 0 <= k < BLOCKS

                def expert(k, n):
                    if held is not None:
                        return held[n + 1]
                    return pe.value_load(eb_i[0:1, k:k + 1], min_val=0, max_val=NE - 1)

                if ok(i + 1):
                    c, q, p = i + 1, (r + 1) % 4, (r + 1) % 2
                    wait(pe, g_x[q], 4 * (c - q) + 16)
                    wait(pe, g_xte, c)
                    for k in range(KD):
                        mm = pe.transpose(bank[0][:, k * P:(k + 1) * P], xg[q][:, k * P:(k + 1) * P], ident)
                    mm.then_inc(g_xt, 1)
                if ok(i - 1):
                    c, p = i - 1, (r - 1) % 2
                    wait(pe, g_h, 2 * c + 2)
                    wait(pe, g_hte, 2 * c)
                    for k in range(KF):
                        mm = pe.transpose(bank[3 + k // 4][:, (k % 4) * P:(k % 4 + 1) * P],
                                          h_sb[p][:, k * P:(k + 1) * P], ident)
                    mm.then_inc(g_ht, 1)
                if ok(i):
                    c, p = i, r % 2
                    wait(pe, g_xte, c + 1)
                    wait(pe, g_hb, 2 * (c - 1))
                    e = expert(c, r)
                    for n in range(2):
                        for k in range(KD):
                            mm = pe.matmul(bank[(1, 6)[p] + n][:, :], xgT[p][:, k, :],
                                           w1_sb[:, bass.ds(e, 1), k, n * 512:(n + 1) * 512]
                                           .rearrange("p o f -> p (o f)"), start=(k == 0), stop=(k == KD - 1))
                        mm.then_inc(g_w1, 1)
                if ok(i - 1):
                    c, p = i - 1, (r - 1) % 2
                    wait(pe, g_hte, 2 * c + 2)
                    wait(pe, g_r, 4 * (c - 1) + 1)
                    e = expert(c, r - 1)
                    for k in range(KF):
                        mm = pe.matmul(bank[5][:, 0:D], hT[:, k, :], w2_sb[:, bass.ds(e, 1), k, :]
                                       .rearrange("p o d -> p (o d)"), start=(k == 0), stop=(k == KF - 1))
                    mm.then_inc(g_w2, 1)

            block_steps(pe, bstep, -1, BLOCKS + 1, experts)

        @block.scalar
        def _(act):
            act.wait_ge(s_param, 48)
            act.activation(negA, negA, ACT.Exp).then_inc(s_negA, 1)
            def pre_pair(pair, r):
                act.wait_ge(s_pre_t, pair + 1)
                wait(act, s_pre_dt, pair - 1)
                act.copy(pre_uT[r % 2].rearrange("p k t -> p (k t)"), bank[r % 2][:, :]).then_inc(s_pre_ev, 1)

            pre_steps(act, pre_pair)
            for e in range(NE - LATE):
                act.dma_start(w1_sb[:, e, :, :], w1[e].rearrange("(k p) f -> p k f", p=P)).then_inc(s_early, 16)
                act.dma_start(w2_sb[:, e, :, :], w2[e].rearrange("(k p) d -> p k d", p=P)).then_inc(s_early, 16)
            act.wait_ge(s_sp, 2)
            act.activation(dta, dta, ACT.Exp, scale=-1.0).then_inc(s_spx, 1)
            act.wait_ge(s_sums, 1)
            flat = lambda v: v.rearrange("p c h -> p (c h)")
            act.activation(flat(e_all), bank[3][:, 0:NC * NH], ACT.Exp).then_inc(s_sumx, 1)
            act.activation(flat(dd_all), bank[4][:, 0:NC * NH], ACT.Exp).then_inc(s_sumx, 1)
            act.activation(flat(cd_all), bank[5][:, 0:NC * NH], ACT.Exp).then_inc(s_sumx, 1)
            act.wait_ge(s_pre, 1)
            act.wait_ge(s_fill, FILLS)

            def step(t, par):
                c, p = t - 3, 1 - par
                if on(c):
                    wait(act, q_yt, c + 1)
                    wait(act, q_op, c)
                    act.copy(yT.rearrange("p k t -> p (k t)"), bank[2][:, :]).then_inc(q_yte, 1)
                c, p = t, par
                if on(c):
                    wait(act, q_inx, c + 1)
                    wait(act, q_halo, c - 1)
                    for n in range(2):
                        act.copy(xbc[p][:, 3 * n:3 * n + 3, TAPS - 1:], bank[n][:, 0:3 * P]
                                 .rearrange("p (m t) -> p m t", m=3)).then_inc(q_xbe, 1)
                c, p = t - 1, 1 - par
                if on(c):
                    wait(act, q_xt, c + 1)
                    wait(act, q_xdt, c - 1)
                    wait(act, q_xd, c - 1)
                    act.copy(x_sb[p].rearrange("p h d -> p (h d)"), bank[4][:, :]).then_inc(q_xte, 1)
                    wait(act, q_bc, c + 1)
                    wait(act, q_st, c - 1)
                    act.copy(b_sb[p], bank[7][:, 0:P]).then_inc(q_be, 1)
                    wait(act, q_seg, c + 1)
                    wait(act, q_y, c - 1)
                    for n in range(2):
                        mm = act.activation(em[p][:, 4 * n:4 * n + 4, :].rearrange("p h l -> p (h l)"), bank[5 + n][:, :], ACT.Exp)
                    mm.then_inc(q_exp, 1)
                c, p = t, par
                if on(c):
                    wait(act, q_conv, 24 * c + 24)
                    wait(act, q_y, c - 1)
                    act.activation(xs[p], cv[p], ACT.Silu).then_inc(q_silx, 1)
                c, p = t - 1, 1 - par
                if on(c):
                    wait(act, q_inz, c + 1)
                    wait(act, q_yv, 4 * (c - 1))
                    act.activation(zs[p], bank[2][:, :], ACT.Silu).then_inc(q_silz, 1)
                c, p = t - 2, par
                if on(c):
                    wait(act, q_yv, 4 * c + 4)
                    wait(act, q_rms, 2 * (c - 1))
                    wait(act, q_sq, c)
                    act.activation(junk, y[p].rearrange("p h d -> p (h d)"), ACT.Square,
                                   accum_out=ssq[:, p:p + 1]).then_inc(q_sq, 1)
                c, p = t - 4, par
                if on(c):
                    wait(act, q_rt, c + 1)
                    wait(act, q_lg, c)
                    act.copy(x1T.rearrange("p k t -> p (k t)"), bank[3][:, 0:D]).then_inc(q_rte, 1)
                c, p = t + 1, 1 - par
                if on(c):
                    wait(act, q_ut, c + 1)
                    wait(act, q_inz, c - 1)
                    act.copy(uT[p].rearrange("p k t -> p (k t)"), bank[5][:, 0:D]).then_inc(q_ute, 1)

            mamba_steps(act, step, -1)

            act.wait_ge(s_rv, 2)
            act.activation(ex, lt, ACT.Exp).then_inc(s_rx, 1)
            act.wait_ge(s_route, 1)

            def bstep(i, r, held):
                ok = lambda k: not isinstance(k, int) or 0 <= k < BLOCKS
                if ok(i + 1):
                    c, p = i + 1, (r + 1) % 2
                    wait(act, g_xt, c + 1)
                    wait(act, g_w1, 2 * (c - 1))
                    act.copy(xgT[p].rearrange("p k t -> p (k t)"), bank[0][:, 0:D]).then_inc(g_xte, 1)
                if ok(i - 1):
                    c, p = i - 1, (r - 1) % 2
                    wait(act, g_ht, c + 1)
                    wait(act, g_w2, c)
                    for n in range(2):
                        act.copy(hT[:, 4 * n:4 * n + 4, :].rearrange("p k t -> p (k t)"), bank[3 + n][:, :]).then_inc(g_hte, 1)
                if ok(i):
                    c, p = i, r % 2
                    for n in range(2):
                        wait(act, g_hb, 2 * c + n + 1)
                        wait(act, g_ht, c - 1)
                        act.activation(h_sb[p][:, n * 512:(n + 1) * 512], hp[p][:, n * 512:(n + 1) * 512],
                                       ACT.Gelu).then_inc(g_h, 1)

            block_steps(act, bstep, -1, BLOCKS + 1)

        @block.vector
        def _(dve):
            dve.wait_ge(s_pre_dt, NC // 2)
            n = [0]

            def sp_step(ins):
                n[0] += 1
                ins.then_inc(s_sp, 1)
                dve.wait_ge(s_sp, n[0])

            psum_dt = bank[2][:, 0:NC * NH].rearrange("p (c h) -> p c h", h=NH)
            sp_step(dve.tensor_tensor(dtx, psum_dt, dtb_row.unsqueeze(1).broadcast_to([P, NC, NH]), ALU.add))
            sp_step(dve.scalar_tensor_tensor(out=dta, in0=dtx, scalar=-1.0, in1=dtx, op0=ALU.mult, op1=ALU.max))
            dve.wait_ge(s_spx, 1)
            sp_step(dve.tensor_scalar(dts, dta, 2.0, None, ALU.add))
            sp_step(dve.reciprocal(dts, dts))
            sp_step(dve.tensor_tensor(dts, dts, dta, ALU.mult))
            sp_step(dve.tensor_tensor(dtq, dts, dts, ALU.mult))
            sp_step(dve.tensor_scalar(dtp, dtq, 1.0 / 19, None, ALU.mult))
            for k in range(17, 1, -2):
                sp_step(dve.scalar_tensor_tensor(out=dtp, in0=dtp, scalar=1.0 / k, in1=dtq, op0=ALU.add, op1=ALU.mult))
            sp_step(dve.scalar_tensor_tensor(out=dtp, in0=dtp, scalar=1.0, in1=dts, op0=ALU.add, op1=ALU.mult))
            sp_step(dve.tensor_scalar(dtx, dtx, 0.0, None, ALU.max))
            sp_step(dve.scalar_tensor_tensor(out=dt_all, in0=dtp, scalar=2.0, in1=dtx, op0=ALU.mult, op1=ALU.add))
            dve.wait_ge(s_negA, 1)
            sp_step(dve.tensor_scalar(negA, negA, -1.0, None, ALU.mult))
            sp_step(dve.tensor_tensor(a_all, dt_all, negA.unsqueeze(1).broadcast_to([P, NC, NH]), ALU.mult))
            assert n[0] == SP_STEPS, n[0]
            dve.wait_ge(s_sumx, 2)
            dve.tensor_tensor(dd_all, dd_all, dt_all, ALU.mult).then_inc(s_pre, 1)
            dve.wait_ge(s_param2, 96)
            for k in range(KI):
                mm = dve.tensor_scalar(w_out[:, k, :], w_out[:, k, :], nw_col[:, k:k + 1], None, ALU.mult)
            mm.then_inc(s_wout, 1)
            dve.wait_ge(s_sumx, 3)
            dve.wait_ge(s_pre, 1)
            dve.wait_ge(s_fill, FILLS)

            def heads(all_chunks, c, n=HD):
                return (all_chunks[:, bass.ds(c, 1), :].rearrange("p o h -> p (o h)").unsqueeze(2)
                        .broadcast_to([P, NH, n]))

            def step(t, par):
                c, p = t, par
                if on(c):
                    wait(dve, q_seg, c - 1)
                    dve.tensor_tensor(ub[p], heads(a_all, c, P), masks[:, M_LE, :].unsqueeze(1).broadcast_to([P, NH, P]),
                                      ALU.mult).then_inc(q_ub, 1)
                c, p = t - 3, 1 - par
                if on(c):
                    wait(dve, q_op, c + 1)
                    wait(dve, q_rms, 2 * c + 2)
                    wait(dve, s_ures[p], 8 * (c - p) + 16)
                    dve.scalar_tensor_tensor(out=u_res[p], in0=bank[3][:, 0:D], scalar=rms[:, p:p + 1], in1=u_res[p],
                                             op0=ALU.mult, op1=ALU.add).then_inc(q_r, 1)
                    wait(dve, q_r, 3 * c + 1)
                    dve.bn_stats(bst[p], u_res[p]).then_inc(q_r, 1)
                    wait(dve, q_r, 3 * c + 2)
                    wait(dve, q_rstd, 2 * (c - 1))
                    settled(dve, s_dve_turns)
                    dve.bn_aggr(mv[p], bst[p]).then_inc(q_r, 1)
                c, p = t, par
                if on(c):
                    wait(dve, q_xbe, 2 * c + 2)
                    wait(dve, q_silx, c - 1)
                    for k in range(TAPS):
                        for m in range(XT_TILES):
                            src = xbc[p][:, m, k:k + P]
                            if k == 0:
                                ins = dve.tensor_scalar(cv[p][:, m, :], src, cw_sb[:, m, 0:1], cb_sb[:, m:m + 1],
                                                        ALU.mult, ALU.add)
                            else:
                                if m == 0:
                                    wait(dve, q_conv, 24 * c + 6 * k)
                                ins = dve.scalar_tensor_tensor(out=cv[p][:, m, :], in0=src, scalar=cw_sb[:, m, k:k + 1],
                                                               in1=cv[p][:, m, :], op0=ALU.mult, op1=ALU.add)
                            ins.then_inc(q_conv, 1)
                    wait(dve, q_conv, 24 * c + 24)
                    dve.tensor_copy(xbc[p][:, :, 0:TAPS - 1], xbc[p][:, :, P:P + TAPS - 1]).then_inc(q_halo, 1)
                c, p = t - 1, 1 - par
                if on(c):
                    wait(dve, q_xte, c + 1)
                    wait(dve, q_y, c - 1)
                    dve.tensor_tensor(xdt[p], x_sb[p], heads(dt_all, c), ALU.mult).then_inc(q_xdt, 1)
                    wait(dve, q_bc, c + 1)
                    wait(dve, q_be, c + 1)
                    dve.tensor_tensor(cbm[p], bank[7][:, P:2 * P], masks[:, M_LE, :], ALU.mult).then_inc(q_cbm, 1)
                    wait(dve, q_exp, c + 1)
                    wait(dve, q_cbm, c + 1)
                    dve.tensor_tensor(em[p], em[p], cbm[p].unsqueeze(1).broadcast_to([P, NH, P]),
                                      ALU.mult).then_inc(q_m, 1)
                c, p = t - 2, par
                if on(c):
                    wait(dve, q_y, c + 1)
                    wait(dve, q_yt, c - 1)
                    wait(dve, q_sq, c - 1)
                    dve.tensor_tensor(y[p], bank[1][:, :].rearrange("p (h d) -> p h d", h=NH), heads(e_all, c),
                                      ALU.mult).then_inc(q_yv, 1)
                    wait(dve, q_yv, 4 * c + 1)
                    dve.tensor_tensor(y[p], bank[0][:, :].rearrange("p (h d) -> p h d", h=NH), y[p],
                                      ALU.add).then_inc(q_yv, 1)
                    wait(dve, q_yv, 4 * c + 2)
                    wait(dve, q_xd, c + 1)
                    dve.tensor_tensor(y[p], y[p], xD[p], ALU.add).then_inc(q_yv, 1)
                    wait(dve, q_yv, 4 * c + 3)
                    wait(dve, q_silz, c + 1)
                    dve.tensor_tensor(y[p].rearrange("p h d -> p (h d)"), y[p].rearrange("p h d -> p (h d)"), zs[p],
                                      ALU.mult).then_inc(q_yv, 1)
                    wait(dve, q_st, c + 1)
                    wait(dve, q_s, 8 * (c - 1))
                    for h in range(NH):
                        dve.scalar_tensor_tensor(out=state[p][:, h, :], in0=state[p][:, h, :],
                                                 scalar=cd_all[:, bass.ds(c, 1), h], in1=bank[4][:, h * HD:(h + 1) * HD],
                                                 op0=ALU.mult, op1=ALU.add).then_inc(q_s, 1)
                c, p = t - 3, 1 - par
                if on(c):
                    wait(dve, q_rstd, 2 * c + 2)
                    dve.tensor_scalar(u_res[p], u_res[p], mv[p][:, 0:1], rstd[:, p:p + 1], ALU.subtract,
                                      ALU.mult).then_inc(q_x1, 1)
                c, p = t - 4, par
                if on(c):
                    wait(dve, q_lg, c + 1)
                    dve.tensor_copy(logits[:, bass.ds(c, 1), :].rearrange("p o e -> p (o e)"), bank[7][:, 0:NE]
                                    ).then_inc(q_lge, 1)

            mamba_steps(dve, step, 0)

            dve.wait_ge(q_lge, NC)
            dve.wait_ge(q_x1, NC)
            r = [0]

            def rv(ins):
                r[0] += 1
                ins.then_inc(s_rv, 1)
                dve.wait_ge(s_rv, r[0])

            over_e = lambda v: v.unsqueeze(2).broadcast_to([P, NC, NE])
            mx, sm, prob, ms, pos, slot, blk, blk_id, tmp = (small[:, k, :] for k in range(9))
            tmp_i, slot_i, blk_i = (small[:, k, :].bitcast(I32) for k in range(9, 12))
            rv(dve.tensor_reduce(mx, logits, AX, ALU.max))
            rv(dve.tensor_tensor(lt, logits, over_e(mx), ALU.subtract))
            dve.wait_ge(s_rx, 1)
            rv(dve.tensor_reduce(sm, ex, AX, ALU.add))
            rv(dve.tensor_reduce(mx, ex, AX, ALU.max))
            rv(dve.tensor_tensor(lt, ex, over_e(mx), ALU.is_equal))
            rv(dve.tensor_tensor(lt, lt, prio.unsqueeze(1).broadcast_to([P, NC, NE]), ALU.mult))
            rv(dve.tensor_reduce(ms, lt, AX, ALU.max))
            rv(dve.tensor_tensor(onehot, lt, over_e(ms), ALU.is_equal))
            assert r[0] == ROUTE_ONEHOT
            rv(dve.reciprocal(prob, sm))
            dve.wait_ge(s_rp, 1)
            rv(dve.tensor_copy(pref[0].rearrange("p c e -> p (c e)"), bank[1][:, 0:NC * NE]))
            rv(dve.tensor_copy(ex.rearrange("p c e -> p (c e)"), bank[1][:, 0:NC * NE]))
            a, d = 0, 1
            while d < NC:
                rv(dve.tensor_copy(pref[1 - a][:, 0:d, :], pref[a][:, 0:d, :]))
                rv(dve.tensor_tensor(pref[1 - a][:, d:, :], pref[a][:, d:, :], pref[a][:, :NC - d, :], ALU.add))
                a, d = 1 - a, 2 * d
            blocks_i, blocks, end0, end1, start = (tiny[:, k, :] for k in range(5))
            rv(dve.tensor_scalar(blocks, pref[a][:, NC - 1, :], float(P - 1), None, ALU.add))
            rv(dve.tensor_copy(blocks_i.bitcast(I32), blocks))
            rv(dve.tensor_scalar(blocks_i.bitcast(I32), blocks_i.bitcast(I32), 7, None, ALU.logical_shift_right))
            rv(dve.tensor_copy(blocks, blocks_i.bitcast(I32)))
            rv(dve.tensor_copy(end0, blocks))
            ends, d = [end0, end1], 1
            while d < NE:
                rv(dve.tensor_copy(ends[1][:, 0:d], ends[0][:, 0:d]))
                rv(dve.tensor_tensor(ends[1][:, d:], ends[0][:, d:], ends[0][:, :NE - d], ALU.add))
                ends, d = ends[::-1], 2 * d
            end = ends[0]
            rv(dve.tensor_tensor(start, end, blocks, ALU.subtract))
            rv(dve.tensor_scalar(start, start, float(P), None, ALU.mult))
            rv(dve.tensor_tensor(lt, pref[a], ex, ALU.subtract))
            rv(dve.tensor_tensor(lt, lt, start.unsqueeze(1).broadcast_to([P, NC, NE]), ALU.add))
            rv(dve.tensor_tensor(lt.rearrange("p c e -> p (c e)"), bank[0][:, 0:NC * NE],
                                 lt.rearrange("p c e -> p (c e)"), ALU.add))
            rv(dve.tensor_tensor(lt, lt, onehot, ALU.mult))
            rv(dve.tensor_reduce(pos, lt, AX, ALU.add))
            rv(dve.tensor_copy(tmp_i, pos))
            rv(dve.tensor_scalar(slot_i, tmp_i, P - 1, None, ALU.bitwise_and))
            rv(dve.tensor_scalar(blk_i, tmp_i, 7, None, ALU.logical_shift_right))
            rv(dve.tensor_copy(slot, slot_i))
            rv(dve.tensor_copy(blk, blk_i))
            rv(dve.tensor_tensor(ge, iota_blk.unsqueeze(2).broadcast_to([P, BLOCKS, NE]),
                                 end.unsqueeze(1).broadcast_to([P, BLOCKS, NE]), ALU.is_ge))
            rv(dve.tensor_reduce(eb_f, ge, AX, ALU.add))
            rv(dve.tensor_scalar(eb_f, eb_f, float(NE - 1), None, ALU.min))
            rv(dve.tensor_copy(eb_i, eb_f))
            for g in range(NC // GT):
                if g:
                    dve.wait_ge(s_inv, g)
                sl = slice(GT * g, GT * g + GT)
                for k in range(GT):
                    ins = dve.tensor_scalar(oh_slot[:, k, :], iota_slot, slot[:, GT * g + k:GT * g + k + 1],
                                            None, ALU.is_equal)
                ins.then_inc(s_ohs, 1)
                for k in range(GT):
                    c = GT * g + k
                    ins = dve.tensor_scalar(oh_blk[:, 0, k, :], iota_blk, blk[:, c:c + 1], ids1[:, c:c + 1],
                                            ALU.is_equal, ALU.mult)
                ins.then_inc(s_ohs, 1)
                for k in range(GT):
                    c = GT * g + k
                    ins = dve.tensor_scalar(oh_blk[:, 1, k, :], iota_blk, blk[:, c:c + 1], prob[:, c:c + 1],
                                            ALU.is_equal, ALU.mult)
                ins.then_inc(s_ohs, 1)
            dve.wait_ge(s_inv, NC // GT)
            rv(dve.tensor_scalar(idx_z, bank[2][:, 0:BLOCKS], 0.0, float(T + 1), ALU.is_equal, ALU.mult))
            rv(dve.scalar_tensor_tensor(out=idx_f, in0=bank[2][:, 0:BLOCKS], scalar=-1.0, in1=idx_z,
                                        op0=ALU.add, op1=ALU.add))
            rv(dve.tensor_copy(prob_blk, bank[2][:, BLOCKS:2 * BLOCKS]))
            dve.tensor_copy(idx_i, idx_f).then_inc(s_route, 1)
            dve.wait_ge(s_route, 1)
            dve.wait_ge(s_late, 32 * LATE + 32)

            def experts(j):
                return [dve.value_load(eb_i[0:1, bass.ds(4 * j + r, 1)], min_val=0, max_val=NE - 1)
                        for r in range(-1, 4)]

            def bstep(i, r, held):
                ok = lambda k: not isinstance(k, int) or 0 <= k < BLOCKS

                def expert(k, n):
                    if held is not None:
                        return held[n + 1]
                    return dve.value_load(eb_i[0:1, k:k + 1], min_val=0, max_val=NE - 1)

                if ok(i):
                    c, p = i, r % 2
                    e = expert(c, r)
                    for n in range(2):
                        wait(dve, g_w1, 2 * c + n + 1)
                        wait(dve, g_h, 2 * (c - 1))
                        dve.tensor_tensor(hp[p][:, n * 512:(n + 1) * 512], bank[(1, 6)[p] + n][:, :],
                                          b1_rep[:, bass.ds(e, 1), n * 512:(n + 1) * 512].rearrange("p o f -> p (o f)"),
                                          ALU.add).then_inc(g_hb, 1)
                if ok(i - 1):
                    c, q, p = i - 1, (r - 1) % 4, (r - 1) % 2
                    wait(dve, g_w2, c + 1)
                    wait(dve, g_out[q], 4 * (c - q))
                    e = expert(c, r - 1)
                    dve.tensor_tensor(yo[q], bank[5][:, 0:D], b2_rep[:, bass.ds(e, 1), :].rearrange("p o d -> p (o d)"),
                                      ALU.add).then_inc(g_r, 1)
                    wait(dve, g_r, 4 * c + 1)
                    dve.scalar_tensor_tensor(out=yo[q], in0=yo[q], scalar=prob_blk[:, bass.ds(c, 1)], in1=xg[q],
                                             op0=ALU.mult, op1=ALU.add).then_inc(g_r, 1)
                    wait(dve, g_r, 4 * c + 2)
                    dve.bn_stats(st2[p], yo[q]).then_inc(g_r, 1)
                    wait(dve, g_r, 4 * c + 3)
                    wait(dve, g_rs, 2 * (c - 1))
                    settled(dve, s_dve_turns)
                    dve.bn_aggr(mv2[p], st2[p]).then_inc(g_r, 1)
                if ok(i - 1):
                    c, q, p = i - 1, (r - 1) % 4, (r - 1) % 2
                    wait(dve, g_rs, 2 * c + 2)
                    dve.tensor_scalar(yo[q], yo[q], mv2[p][:, 0:1], rstd2[p][:, 1:2], ALU.subtract,
                                      ALU.mult).then_inc(g_y, 1)

            block_steps(dve, bstep, 0, BLOCKS + 1, experts)


_INS = ["L0_attn_u", "L0_attn_in_proj_w", "L0_attn_conv_weight", "L0_attn_conv_bias", "L0_attn_dt_bias",
        "L0_attn_A_log", "L0_attn_D_param", "L0_attn_norm_weight", "L0_attn_out_proj_w",
        "L0_ffn_Wr", "L0_ffn_W1", "L0_ffn_b1", "L0_ffn_W2", "L0_ffn_b2"]


def kernel(**inputs):
    import concourse.bacc as bacc
    from concourse.bass_utils import run_bass_kernel_spmd as run

    nc = bacc.Bacc("TRN2", target_bir_lowering=False, num_devices=1)
    arrays, args = {}, []
    channels = lambda a: a.reshape(a.shape[0] // P, P, -1).swapaxes(0, 1)
    for name in _INS:
        a = np.asarray(inputs[name])
        if name.endswith("conv_weight"):
            a = channels(a)
        elif name.endswith(("conv_bias", "norm_weight")):
            a = channels(a)[:, :, 0]
        a = np.ascontiguousarray(a)
        arrays[f"in_{name}"] = a
        args.append(nc.dram_tensor(f"in_{name}", a.shape, mybir.dt.from_np(a.dtype), kind="ExternalInput").ap())
    arrays["in_constants"] = constants()
    args.append(nc.dram_tensor("in_constants", (P, CW), F32, kind="ExternalInput").ap())
    out = nc.dram_tensor("out", (T, D), F32, kind="ExternalOutput").ap()
    build(nc, *args, out)
    r = run(nc, [arrays], core_ids=[0])
    return r.results[0]["out"].reshape(NB, L, D)
```

```python
from contextlib import ExitStack

import numpy as np

import concourse.bass as bass
from concourse import mybir

ALU = mybir.AluOpType
ACT = mybir.ActivationFunctionType
AX = mybir.AxisListType.X
F32 = mybir.dt.float32
I32 = mybir.dt.int32

P = 128
NB, L, D = 2, 2048, 256
DI, NS, NH, HD = 512, 128, 8, 64
TAPS = 4
NPROJ = 2 * DI + 2 * NS + NH
XT_TILES = (DI + 2 * NS) // P
XD_TILES = DI // P
NE, FF = 8, 1024
EPS = 1e-5
T = NB * L
NC = T // P
BLOCKS = T // P + NE
LATE = 3
KD, KF, KI = D // P, FF // P, DI // P

M_ID, M_LE, M_GT, M_LT = range(4)
N_MASKS = 4
CW = N_MASKS * P + BLOCKS + NE + NC + P
FILLS = 7
CONV = (TAPS - 1) * XT_TILES
SP_STEPS = 20
ROUTE_ONEHOT = 8


def constants():
    k, m = np.arange(P)[:, None], np.arange(P)[None, :]
    masks = [k == m, k <= m, k > m, k < m]
    c, rest = np.zeros((P, CW), np.float32), N_MASKS * P
    for n, mask in enumerate(masks):
        c[:, n * P:(n + 1) * P] = mask
    c[:, rest:rest + BLOCKS] = np.arange(BLOCKS)
    c[:, rest + BLOCKS:rest + BLOCKS + NE] = NE - np.arange(NE)
    chunk = np.arange(NC)
    c[:, rest + BLOCKS + NE:CW - P] = (chunk % NB) * L + (chunk // NB) * P + k + 1
    c[:, CW - P:] = np.arange(P)
    return c


def wait(eng, sem, n):
    if not isinstance(n, int) or n > 0:
        eng.wait_ge(sem, n)


def settled(eng, turns):
    eng.sem_inc(turns, 1)


def edge(eng, sem, c, n):
    if isinstance(c, int):
        wait(eng, sem, n)


def on(c):
    return not isinstance(c, int) or 0 <= c < NC


def mamba_steps(eng, step, first):
    peeled, lag = 8, 6
    for t in range(first, peeled):
        step(t, t % 2)
    with eng.Fori(peeled // 2, NC // 2 - 1) as j:
        for par in range(2):
            step(2 * j + par, par)
    for t in range(NC - 2, NC + lag):
        step(t, t % 2)


def pre_steps(eng, pair_step):
    for pair in range(4):
        pair_step(pair, pair)
    with eng.Fori(1, NC // 8) as q:
        for r in range(4):
            pair_step(4 * q + r, r)


def block_steps(eng, step, first, last, before=None):
    for i in range(first, 8):
        step(i, i % 4, None)
    with eng.Fori(2, BLOCKS // 4 - 1) as j:
        held = before(j) if before else None
        for r in range(4):
            step(4 * j + r, r, held)
    for i in range(BLOCKS - 4, last):
        step(i, i % 4, None)


def build(nc, u, in_proj_w, conv_w, conv_b, dt_bias, a_log, d_param, norm_w, out_proj_w,
          wr, w1, b1, w2, b2, consts, out):
    x1_rows = nc.dram_tensor("x1_rows", [T + 1, D], F32, kind="Internal").ap()
    ctx = ExitStack()
    with ctx:
        wsize = KD * FF + KF * D
        wtotal = NE * wsize
        arena = ctx.enter_context(nc.sbuf_tensor("arena", [P, 53100], F32))
        at = [0]

        def carve(*shape):
            n = int(np.prod(shape))
            v = arena[:, at[0]:at[0] + n]
            at[0] += n
            if len(shape) == 2:
                v = v.rearrange("p (a b) -> p a b", a=shape[0])
            elif len(shape) == 3:
                v = v.rearrange("p (a b c) -> p a b c", a=shape[0], b=shape[1])
            return v

        w1_sb = arena[:, 0:NE * KD * FF].rearrange("p (e k f) -> p e k f", e=NE, k=KD)
        w2_sb = arena[:, NE * KD * FF:wtotal].rearrange("p (e k d) -> p e k d", e=NE, k=KF)
        at[0] = wtotal
        cst = carve(CW)
        masks = cst[:, 0:N_MASKS * P].rearrange("p (n m) -> p n m", n=N_MASKS)
        ident = masks[:, M_ID, :]
        iota_blk = cst[:, N_MASKS * P:N_MASKS * P + BLOCKS]
        prio = cst[:, N_MASKS * P + BLOCKS:N_MASKS * P + BLOCKS + NE]
        ids1 = cst[:, N_MASKS * P + BLOCKS + NE:CW - P]
        iota_slot = cst[:, CW - P:CW]
        ones = carve(P)
        half_neg = carve(2)
        logits = carve(NC, NE)
        wr_sb = carve(KD, NE)
        zrow = carve(D)
        persistent_end = at[0]

        b1_rep = carve(NE, FF)
        b2_rep = carve(NE, D)
        idx_f = carve(BLOCKS)
        idx_z = carve(BLOCKS)
        idx_i = carve(BLOCKS).bitcast(I32)
        prob_blk = carve(BLOCKS)
        eb_f = carve(BLOCKS)
        eb_i = carve(BLOCKS).bitcast(I32)
        idx_col = [carve(1).bitcast(I32) for _ in range(4)]
        idx_out = [carve(1).bitcast(I32) for _ in range(4)]
        temp_start = at[0]
        xg = [carve(D) for _ in range(4)]
        yo = [carve(D) for _ in range(4)]
        xgT = [carve(KD, P) for _ in range(2)]
        hp = [carve(FF) for _ in range(2)]
        h_sb = [carve(FF) for _ in range(2)]
        hT = carve(KF, P)
        st2 = [carve(6) for _ in range(2)]
        mv2 = [carve(2) for _ in range(2)]
        rstd2 = [carve(2) for _ in range(2)]
        assert at[0] <= 53100
        at[0] = temp_start
        lt = carve(NC, NE)
        ex = carve(NC, NE)
        onehot = carve(NC, NE)
        pref = [carve(NC, NE) for _ in range(2)]
        small = carve(16, NC)
        GT = 4
        oh_slot = carve(GT, P)
        oh_blk = carve(2, GT, BLOCKS)
        ge = carve(BLOCKS, NE)
        tiny = carve(16, NE)
        assert at[0] <= 53100, at[0]

        at[0] = persistent_end
        w_in = carve(KD, NPROJ)
        w_out = carve(KI, D)
        nw_col = carve(KI)
        cw_sb = carve(XT_TILES, TAPS)
        cb_sb = carve(XT_TILES)
        d_row = carve(NH)
        dtb_row = carve(NH)
        negA = carve(NH)
        a_all = carve(NC, NH)
        dt_all = carve(NC, NH)
        e_all = carve(NC, NH)
        cd_all = carve(NC, NH)
        dd_all = carve(NC, NH)
        u_in = [carve(D) for _ in range(2)]
        uT = [carve(KD, P) for _ in range(2)]
        u_res = [carve(D) for _ in range(2)]
        xs = [carve(XT_TILES, P) for _ in range(2)]
        zs = [carve(DI) for _ in range(2)]
        xdt = [carve(NH, HD) for _ in range(2)]
        state = [carve(NH, HD) for _ in range(2)]
        sdec = [carve(NH, HD) for _ in range(2)]
        y = [carve(NH, HD) for _ in range(2)]
        yT = carve(KI, P)
        x1T = carve(KD, P)
        cbm = [carve(P) for _ in range(2)]
        b_sb = [carve(P) for _ in range(2)]
        ssq = carve(2)
        rms = carve(2)
        bst = [carve(6) for _ in range(2)]
        mv = [carve(2) for _ in range(2)]
        rstd = carve(2)
        assert at[0] <= 53100, at[0]
        at[0] = NE * KD * FF + (NE - LATE) * KF * D
        xbc = [carve(XT_TILES, TAPS - 1 + P) for _ in range(2)]
        cv = [carve(XT_TILES, P) for _ in range(2)]
        x_sb = [carve(NH, HD) for _ in range(2)]
        xdd = [carve(NH, HD) for _ in range(2)]
        assert at[0] <= wtotal, (at[0], wtotal)
        at[0] = (NE - LATE) * KD * FF
        ub = [carve(NH, P) for _ in range(2)]
        em = [carve(NH, P) for _ in range(2)]
        junk = carve(DI)
        touch = carve(1)
        xD = [carve(NH, HD) for _ in range(2)]
        assert at[0] <= NE * KD * FF
        at[0] = (NE - LATE) * KD * FF
        pre_u = [carve(NB, D) for _ in range(4)]
        pre_uT = [carve(NB * KD, P) for _ in range(2)]
        dtx = carve(NC, NH)
        dta = carve(NC, NH)
        dts = carve(NC, NH)
        dtq = carve(NC, NH)
        dtp = carve(NC, NH)
        assert at[0] <= NE * KD * FF

        bank = [ctx.enter_context(nc.psum_tensor(f"bank{n}", [P, 512], F32)) for n in range(8)]

        def sem(name):
            return ctx.enter_context(nc.semaphore(name))

        s_const = sem("const_loaded")
        s_param = sem("dt_params_loaded")
        s_param2 = sem("mamba_params_loaded")
        s_early = sem("early_experts_loaded")
        s_late = sem("late_experts_loaded")
        s_zrow = sem("zero_row_stored")
        s_fill = sem("fills_done")
        s_pool_turns, s_dve_turns, s_sp_turns = sem("pool_turns"), sem("dve_turns"), sem("sp_turns")
        s_wout = sem("out_proj_scaled")
        s_pre_u = [sem(f"pre_u_loaded{n}") for n in range(4)]
        s_pre_t = sem("pre_transposed")
        s_pre_ev = sem("pre_uT_ready")
        s_pre_dt = sem("pre_dt_product")
        s_negA = sem("negA_steps")
        s_sp = sem("softplus_steps")
        s_spx = sem("softplus_exp")
        s_sums = sem("chunk_sums")
        s_sumx = sem("chunk_sums_exp")
        s_pre = sem("dt_phase_done")
        s_uin = [sem(f"u_in_loaded{n}") for n in range(2)]
        s_ures = [sem(f"u_res_loaded{n}") for n in range(2)]
        s_x1st = [sem(f"x1_stored{n}") for n in range(2)]
        q_table = sem("table_touched")
        q_ut, q_ute = sem("u_and_x1_transposed"), sem("uT_and_x1T_ready")
        q_inx, q_xbe, q_tap, q_halo = sem("xbc_product"), sem("xbc_ready"), sem("last_tap_ready"), sem("halo_copied")
        q_conv, q_silx = sem("conv_steps"), sem("xs_ready")
        q_inz, q_silz = sem("z_product"), sem("zs_ready")
        q_xt, q_xte = sem("x_transposed"), sem("x_ready")
        q_bc, q_be, q_cbm = sem("b_and_cb"), sem("b_ready"), sem("cb_masked")
        q_ub, q_seg, q_exp, q_m = sem("a_mask_ready"), sem("segment_sums"), sem("decay_ready"), sem("m_ready")
        q_xdt, q_xdd, q_xd = sem("xdt_ready"), sem("xdd_ready"), sem("xD_ready")
        q_y, q_yv, q_sq = sem("y_products"), sem("y_steps"), sem("y_squared")
        q_st, q_sd, q_s = sem("state_product"), sem("state_decayed"), sem("state_updated")
        q_rms, q_yt, q_yte = sem("rms_steps"), sem("y_transposed"), sem("yT_ready")
        q_op, q_r, q_rstd, q_x1 = sem("out_product"), sem("residual_steps"), sem("rstd_steps"), sem("x1_ready")
        q_lg, q_lge = sem("logit_product"), sem("logits_ready")
        s_rv, s_rx, s_rp, s_ohs, s_inv = (sem("route_steps"), sem("route_exp"), sem("route_products"),
                                          sem("onehots_ready"), sem("slots_product"))
        s_route = sem("routing_done")
        g_idx, g_x = sem("gather_index_ready"), [sem(f"rows_gathered{n}") for n in range(4)]
        g_xt, g_xte = sem("xg_transposed"), sem("xgT_ready")
        g_w1, g_hb, g_h = sem("w1_product"), sem("h_biased"), sem("h_ready")
        g_ht, g_hte, g_w2 = sem("h_transposed"), sem("hT_ready"), sem("w2_product")
        g_r, g_rs, g_y = sem("block_residual_steps"), sem("block_rstd_steps"), sem("block_rows_ready")
        g_oidx, g_out = sem("scatter_index_ready"), [sem(f"rows_scattered{n}") for n in range(4)]

        def chunk_rows(c, par):
            return (c - par) * (P // 2) + par * L

        def heads(all_chunks, c, n=HD):
            return (all_chunks[:, bass.ds(c, 1), :].rearrange("p o h -> p (o h)").unsqueeze(2)
                    .broadcast_to([P, NH, n]))

        block = ctx.enter_context(nc.Block())

        @block.sync
        def _(sp):
            sp.dma_start(w_in[:, :, :], in_proj_w.rearrange("(k p) n -> p k n", p=P)).then_inc(s_param, 16)
            sp.dma_start(cst, consts).then_inc(s_const, 16)
            sp.dma_start(dtb_row, dt_bias.partition_broadcast(P)).then_inc(s_param, 16)
            sp.dma_start(negA, a_log.partition_broadcast(P)).then_inc(s_param, 16)
            def load_pair(pair, r):
                wait(sp, s_pre_t, pair - 3)
                sp.dma_start(pre_u[r], u[:, bass.ds(pair * P, P), :].rearrange("b p d -> p b d")).then_inc(s_pre_u[r], 16)

            pre_steps(sp, load_pair)
            sp.dma_start(w_out[:, :, :], out_proj_w.rearrange("(k p) n -> p k n", p=P)).then_inc(s_param2, 16)
            sp.dma_start(nw_col, norm_w).then_inc(s_param2, 16)
            sp.dma_start(cw_sb[:, :, :], conv_w).then_inc(s_param2, 16)
            sp.dma_start(cb_sb, conv_b).then_inc(s_param2, 16)
            sp.dma_start(d_row, d_param.partition_broadcast(P)).then_inc(s_param2, 16)
            sp.dma_start(wr_sb[:, :, :], wr.rearrange("(k p) e -> p k e", p=P)).then_inc(s_param2, 16)
            sp.wait_ge(s_fill, 1)
            sp.dma_start(x1_rows[T:T + 1, :], zrow[0:1, :]).then_inc(s_zrow, 16)

            def step(t, par):
                if on(t - 5):
                    wait(sp, q_x1, t - 4)
                    settled(sp, s_sp_turns)
                    sp.dma_start(x1_rows[bass.ds(chunk_rows(t - 5, 1 - par), P), :], u_res[1 - par]
                                 ).then_inc(s_x1st[1 - par], 16)
                if on(t + 2):
                    wait(sp, q_ut, t + 1)
                    c = t + 2
                    sp.dma_start(u_in[par], u[par, bass.ds((c - par) * (P // 2), P), :]).then_inc(s_uin[par], 16)
                c, p = t - 3, 1 - par
                if on(c):
                    if not isinstance(t, int) or t >= 5:
                        wait(sp, q_ut, t + 2)
                    wait(sp, s_x1st[p], 8 * (c - 2 - p) + 16)
                    settled(sp, s_sp_turns)
                    sp.dma_start(u_res[p], u[p, bass.ds((c - p) * (P // 2), P), :]).then_inc(s_ures[p], 16)

            mamba_steps(sp, step, -2)

            sp.wait_ge(q_lge, NC)
            sp.wait_ge(q_s, NC)
            sp.wait_ge(q_x1, NC)
            sp.wait_ge(q_sq, NC)
            for e in range(NE - LATE, NE):
                sp.dma_start(w1_sb[:, e, :, :], w1[e].rearrange("(k p) f -> p k f", p=P)).then_inc(s_late, 16)
                sp.dma_start(w2_sb[:, e, :, :], w2[e].rearrange("(k p) d -> p k d", p=P)).then_inc(s_late, 16)
            sp.dma_start(b1_rep[:, :, :].rearrange("p e f -> p (e f)"),
                         b1.rearrange("e f -> (e f)").partition_broadcast(P)).then_inc(s_late, 16)
            sp.dma_start(b2_rep[:, :, :].rearrange("p e f -> p (e f)"),
                         b2.rearrange("e f -> (e f)").partition_broadcast(P)).then_inc(s_late, 16)

        @block.gpsimd
        def _(pool):
            pool.memset(zrow, 0.0).then_inc(s_fill, 1)
            pool.memset(ones, 1.0).then_inc(s_fill, 1)
            pool.memset(half_neg, -0.5).then_inc(s_fill, 1)
            pool.memset(state[0][:, :, :], 0.0).then_inc(s_fill, 1)
            pool.memset(state[1][:, :, :], 0.0).then_inc(s_fill, 1)
            for par in range(2):
                pool.memset(xbc[par][:, :, 0:TAPS - 1], 0.0).then_inc(s_fill, 1)
            pool.wait_ge(s_fill, FILLS)
            pool.wait_ge(s_param2, 96)
            pool.wait_ge(s_pre, 1)
            pool.wait_ge(s_sumx, 3)
            pool.wait_ge(s_sp, SP_STEPS)

            def step(t, par):
                c, p = t - 1, 1 - par
                if on(c):
                    wait(pool, q_xte, c + 1)
                    wait(pool, q_st, c - 1)
                    pool.tensor_tensor(xdd[p], x_sb[p], heads(dd_all, c), ALU.mult).then_inc(q_xdd, 1)
                    wait(pool, q_yv, 4 * (c - 1))
                    pool.tensor_tensor(xD[p], x_sb[p], d_row.unsqueeze(2).broadcast_to([P, NH, HD]),
                                       ALU.mult).then_inc(q_xd, 1)
                c, p = t, par
                if on(c):
                    wait(pool, q_seg, c - 1)
                    pool.tensor_tensor(ub[p], heads(a_all, c, P), masks[:, M_LE, :].unsqueeze(1)
                                       .broadcast_to([P, NH, P]), ALU.mult).then_inc(q_ub, 1)
                c, p = t - 2, par
                if on(c):
                    wait(pool, q_s, c - 1)
                    pool.tensor_tensor(sdec[p], state[p], heads(cd_all, c), ALU.mult).then_inc(q_sd, 1)
                c, p = t - 3, 1 - par
                if on(c):
                    wait(pool, q_sq, c + 1)
                    wait(pool, q_r, 3 * (c - 2) + 1)
                    settled(pool, s_pool_turns)
                    pool.tensor_scalar(rms[:, p:p + 1], ssq[:, p:p + 1], 1.0 / DI, EPS, ALU.mult, ALU.add
                                       ).then_inc(q_rms, 1)
                    wait(pool, q_rms, 2 * c + 1)
                    pool.tensor_tensor(rms[:, p:p + 1], rms[:, p:p + 1], half_neg[:, 0:1], ALU.pow).then_inc(q_rms, 1)
                c, p = t - 4, par
                if on(c):
                    wait(pool, q_r, 3 * c + 3)
                    wait(pool, q_x1, c - 1)
                    settled(pool, s_pool_turns)
                    pool.tensor_scalar(rstd[:, p:p + 1], mv[p][:, 1:2], EPS, None, ALU.add).then_inc(q_rstd, 1)
                    wait(pool, q_rstd, 2 * c + 1)
                    pool.tensor_tensor(rstd[:, p:p + 1], rstd[:, p:p + 1], half_neg[:, 0:1], ALU.pow
                                       ).then_inc(q_rstd, 1)

            mamba_steps(pool, step, 0)

            pool.wait_ge(s_route, 1)
            pool.wait_ge(s_zrow, 16)
            for par in range(2):
                pool.wait_ge(s_x1st[par], 16 * NC // 2)
            limit_in, limit_out = T, T - 1

            def bstep(i, r, held):
                ok = lambda k: not isinstance(k, int) or 0 <= k < BLOCKS
                if ok(i + 2):
                    c, q = i + 2, (r + 2) % 4
                    wait(pool, g_y, c - 3)
                    pool.tensor_copy(idx_col[q], idx_i[:, bass.ds(c, 1)]).then_inc(g_idx, 1)
                    wait(pool, g_idx, c + 1)
                    settled(pool, s_pool_turns)
                    pool.indirect_dma_start(xg[q], None, x1_rows[:, :],
                                            bass.IndirectOffsetOnAxis(ap=idx_col[q], axis=0),
                                            bounds_check=limit_in, oob_is_err=False).then_inc(g_x[q], 16)
                if ok(i - 1):
                    c, q = i - 1, (r - 1) % 4
                    p = (r - 1) % 2
                    wait(pool, g_r, 4 * c + 4)
                    wait(pool, g_y, c - 1)
                    settled(pool, s_pool_turns)
                    pool.tensor_scalar(rstd2[p][:, 0:1], mv2[p][:, 1:2], EPS, None, ALU.add).then_inc(g_rs, 1)
                    wait(pool, g_rs, 2 * c + 1)
                    pool.tensor_tensor(rstd2[p][:, 1:2], rstd2[p][:, 0:1], half_neg[:, 0:1], ALU.pow
                                       ).then_inc(g_rs, 1)
                if ok(i - 2):
                    c, q = i - 2, (r - 2) % 4
                    wait(pool, g_out[q], 4 * (c - q))
                    pool.tensor_copy(idx_out[q], idx_i[:, bass.ds(c, 1)]).then_inc(g_oidx, 1)
                    wait(pool, g_oidx, c + 1)
                    wait(pool, g_y, c + 1)
                    settled(pool, s_pool_turns)
                    pool.indirect_dma_start(out, bass.IndirectOffsetOnAxis(ap=idx_out[q], axis=0), yo[q], None,
                                            bounds_check=limit_out, oob_is_err=False).then_inc(g_out[q], 16)

            block_steps(pool, bstep, -2, BLOCKS + 2)
            for q in range(4):
                pool.wait_ge(g_out[q], 16 * BLOCKS // 4)

        @block.tensor
        def _(pe):
            pe.wait_ge(s_const, 16)
            pe.wait_ge(s_param, 48)
            def pre_pair(pair, r):
                p = r % 2
                pe.wait_ge(s_pre_u[r], 4 * (pair - r) + 16)
                wait(pe, s_pre_ev, pair - 1)
                for b in range(NB):
                    for k in range(KD):
                        mm = pe.transpose(bank[p][:, (b * KD + k) * P:(b * KD + k + 1) * P],
                                          pre_u[r][:, b, k * P:(k + 1) * P], ident)
                mm.then_inc(s_pre_t, 1)
                pe.wait_ge(s_pre_ev, pair + 1)
                for b in range(NB):
                    for k in range(KD):
                        mm = pe.matmul(bank[2][:, bass.ds(pair * (NB * NH) + b * NH, NH)],
                                       pre_uT[p][:, b * KD + k, :], w_in[:, k, NPROJ - NH:NPROJ],
                                       start=(k == 0), stop=(k == KD - 1))
                mm.then_inc(s_pre_dt, 1)

            pre_steps(pe, pre_pair)
            pe.wait_ge(s_sp, SP_STEPS)
            flat = lambda v: v.rearrange("p c h -> p (c h)")
            pe.wait_ge(s_fill, FILLS)
            pe.matmul(bank[3][:, 0:NC * NH], masks[:, M_LE, :], flat(a_all), start=True, stop=True)
            pe.matmul(bank[4][:, 0:NC * NH], masks[:, M_GT, :], flat(a_all), start=True, stop=True)
            pe.matmul(bank[5][:, 0:NC * NH], ones, flat(a_all), start=True, stop=True).then_inc(s_sums, 1)
            pe.wait_ge(s_pre, 1)
            pe.wait_ge(s_sumx, 3)
            pe.wait_ge(s_param2, 96)
            pe.wait_ge(s_wout, 1)

            def turn(c, behind):
                return min(c + behind, NC) if isinstance(c, int) else c + behind

            def step(t, par):
                c, p = t, par
                if on(c):
                    wait(pe, q_ute, c + 1)
                    wait(pe, q_tap, c)
                    for m in range(XT_TILES):
                        lo = DI + m * P
                        for k in range(KD):
                            mm = pe.matmul(bank[m // 3][:, (m % 3) * P:(m % 3 + 1) * P], w_in[:, k, lo:lo + P],
                                           uT[p][:, k, :], start=(k == 0), stop=(k == KD - 1))
                    mm.then_inc(q_inx, 1)
                c, p = t - 1, 1 - par
                if on(c):
                    wait(pe, q_ub, c + 1)
                    wait(pe, q_yv, 4 * (c - 2) + 2)
                    edge(pe, q_exp, c, c)
                    for n in range(2):
                        mm = pe.matmul(bank[5 + n][:, :], masks[:, M_GT, :],
                                       ub[p][:, 4 * n:4 * n + 4, :].rearrange("p h l -> p (h l)"), start=True, stop=True)
                    mm.then_inc(q_seg, 1)
                    wait(pe, q_silx, c + 1)
                    wait(pe, q_s, c - 1)
                    edge(pe, q_xte, c, c)
                    for m in range(XD_TILES):
                        mm = pe.transpose(bank[4][:, m * P:(m + 1) * P], xs[p][:, m, :], ident)
                    mm.then_inc(q_xt, 1)
                    wait(pe, q_be, c)
                    wait(pe, q_cbm, c)
                    pe.transpose(bank[7][:, 0:P], xs[p][:, XD_TILES, :], ident)
                    pe.matmul(bank[7][:, P:2 * P], xs[p][:, XD_TILES, :], xs[p][:, XD_TILES + 1, :],
                              start=True, stop=True).then_inc(q_bc, 1)
                    wait(pe, q_yte, c - 2)
                    edge(pe, q_silz, c, c)
                    for k in range(KD):
                        mm = pe.matmul(bank[2][:, :], uT[p][:, k, :], w_in[:, k, 0:DI], start=(k == 0), stop=(k == KD - 1))
                    mm.then_inc(q_inz, 1)
                if on(t + 1) or on(t - 5):
                    edge(pe, q_ute, t, t + 1)
                    if on(t):
                        wait(pe, q_tap, t + 1)
                    if on(t + 1):
                        wait(pe, s_uin[1 - par], 8 * (t + par) + 16)
                        for k in range(KD):
                            mm = pe.transpose(bank[0][:, k * P:(k + 1) * P], u_in[1 - par][:, k * P:(k + 1) * P], ident)
                    if on(t - 5):
                        wait(pe, q_x1, t - 4)
                        for k in range(KD):
                            mm = pe.transpose(bank[0][:, D + k * P:D + (k + 1) * P], u_res[1 - par][:, k * P:(k + 1) * P],
                                              ident)
                    mm.then_inc(q_ut, 1)
                c, p = t - 4, par
                if on(c):
                    wait(pe, q_yte, c + 1)
                    wait(pe, q_r, 3 * (c - 1) + 1)
                    wait(pe, q_lge, c - 2)
                    for k in range(KI):
                        mm = pe.matmul(bank[3][:, 0:D], yT[:, k, :], w_out[:, k, :], start=(k == 0), stop=(k == KI - 1))
                    mm.then_inc(q_op, 1)
                c, p = t - 6, par
                if on(c):
                    wait(pe, q_ute, t + 1)
                    edge(pe, q_lge, c, c)
                    if isinstance(t, int):
                        wait(pe, q_r, 3 * min(t - 5, NC - 1) + 1)
                    for k in range(KD):
                        mm = pe.matmul(bank[3][:, D:D + NE], x1T[:, k, :], wr_sb[:, k, :], start=(k == 0), stop=(k == KD - 1))
                    mm.then_inc(q_lg, 1)
                c, p = t - 2, par
                if on(c):
                    wait(pe, q_m, c + 1)
                    wait(pe, q_xdt, c + 1)
                    wait(pe, q_exp, turn(c, 2))
                    edge(pe, q_yv, c, 4 * (c - 1) + 2)
                    for h in range(NH):
                        pe.matmul(bank[5][:, h * HD:(h + 1) * HD], em[p][:, h, :], xdt[p][:, h, :], start=True, stop=True)
                    wait(pe, q_s, c - 1)
                    pe.matmul(bank[6][:, :], xs[p][:, XD_TILES + 1, :], state[p].rearrange("p h d -> p (h d)"),
                              start=True, stop=True).then_inc(q_y, 1)
                c, p = t - 3, 1 - par
                if on(c):
                    wait(pe, q_yv, 4 * c + 4)
                    wait(pe, q_silz, turn(c, 3))
                    edge(pe, q_yte, c, c)
                    yf = y[p].rearrange("p h d -> p (h d)")
                    for k in range(KI):
                        mm = pe.transpose(bank[2][:, k * P:(k + 1) * P], yf[:, k * P:(k + 1) * P], ident)
                    mm.then_inc(q_yt, 1)
                c, p = t - 2, par
                if on(c):
                    wait(pe, q_xdd, c + 1)
                    wait(pe, q_be, c + 1)
                    wait(pe, q_xte, turn(c, 2))
                    edge(pe, q_s, c, c)
                    pe.matmul(bank[4][:, :], b_sb[p], xdd[p].rearrange("p h d -> p (h d)"),
                              start=True, stop=True).then_inc(q_st, 1)

            mamba_steps(pe, step, -1)

            pe.wait_ge(s_rv, ROUTE_ONEHOT)
            pe.wait_ge(q_lge, NC)
            pe.matmul(bank[0][:, 0:NC * NE], masks[:, M_LT, :], flat(onehot), start=True, stop=True)
            pe.matmul(bank[1][:, 0:NC * NE], ones, flat(onehot), start=True, stop=True).then_inc(s_rp, 1)
            for c in range(NC):
                if c % GT == 0:
                    pe.wait_ge(s_ohs, 3 * (c // GT + 1))
                mm = pe.matmul(bank[2][:, 0:2 * BLOCKS], oh_slot[:, c % GT, :], oh_blk[:, :, c % GT, :],
                               start=(c == 0), stop=(c == NC - 1))
                if c % GT == GT - 1:
                    mm.then_inc(s_inv, 1)

            pe.wait_ge(s_route, 1)
            pe.wait_ge(s_early, 32 * (NE - LATE))
            pe.wait_ge(s_late, 32 * LATE + 32)

            def experts(j):
                return [pe.value_load(eb_i[0:1, bass.ds(4 * j + r, 1)], min_val=0, max_val=NE - 1)
                        for r in range(-1, 4)]

            def bstep(i, r, held):
                ok = lambda k: not isinstance(k, int) or 0 <= k < BLOCKS

                def expert(k, n):
                    if held is not None:
                        return held[n + 1]
                    return pe.value_load(eb_i[0:1, k:k + 1], min_val=0, max_val=NE - 1)

                if ok(i + 1):
                    c, q, p = i + 1, (r + 1) % 4, (r + 1) % 2
                    wait(pe, g_x[q], 4 * (c - q) + 16)
                    wait(pe, g_xte, c)
                    for k in range(KD):
                        mm = pe.transpose(bank[0][:, k * P:(k + 1) * P], xg[q][:, k * P:(k + 1) * P], ident)
                    mm.then_inc(g_xt, 1)
                if ok(i - 1):
                    c, p = i - 1, (r - 1) % 2
                    wait(pe, g_h, 2 * c + 2)
                    wait(pe, g_hte, 2 * c)
                    for k in range(KF):
                        mm = pe.transpose(bank[3 + k // 4][:, (k % 4) * P:(k % 4 + 1) * P],
                                          h_sb[p][:, k * P:(k + 1) * P], ident)
                    mm.then_inc(g_ht, 1)
                if ok(i):
                    c, p = i, r % 2
                    wait(pe, g_xte, c + 1)
                    wait(pe, g_hb, 2 * (c - 1))
                    e = expert(c, r)
                    for n in range(2):
                        for k in range(KD):
                            mm = pe.matmul(bank[(1, 6)[p] + n][:, :], xgT[p][:, k, :],
                                           w1_sb[:, bass.ds(e, 1), k, n * 512:(n + 1) * 512]
                                           .rearrange("p o f -> p (o f)"), start=(k == 0), stop=(k == KD - 1))
                        mm.then_inc(g_w1, 1)
                if ok(i - 1):
                    c, p = i - 1, (r - 1) % 2
                    wait(pe, g_hte, 2 * c + 2)
                    wait(pe, g_r, 4 * (c - 1) + 1)
                    e = expert(c, r - 1)
                    for k in range(KF):
                        mm = pe.matmul(bank[5][:, 0:D], hT[:, k, :], w2_sb[:, bass.ds(e, 1), k, :]
                                       .rearrange("p o d -> p (o d)"), start=(k == 0), stop=(k == KF - 1))
                    mm.then_inc(g_w2, 1)

            block_steps(pe, bstep, -1, BLOCKS + 1, experts)

        @block.scalar
        def _(act):
            act.wait_ge(s_param, 48)
            act.activation(negA, negA, ACT.Exp).then_inc(s_negA, 1)
            def pre_pair(pair, r):
                act.wait_ge(s_pre_t, pair + 1)
                wait(act, s_pre_dt, pair - 1)
                act.copy(pre_uT[r % 2].rearrange("p k t -> p (k t)"), bank[r % 2][:, :]).then_inc(s_pre_ev, 1)

            pre_steps(act, pre_pair)
            for e in range(NE - LATE):
                act.dma_start(w1_sb[:, e, :, :], w1[e].rearrange("(k p) f -> p k f", p=P)).then_inc(s_early, 16)
                act.dma_start(w2_sb[:, e, :, :], w2[e].rearrange("(k p) d -> p k d", p=P)).then_inc(s_early, 16)
            act.wait_ge(s_sp, 2)
            act.activation(dta, dta, ACT.Exp, scale=-1.0).then_inc(s_spx, 1)
            act.wait_ge(s_sums, 1)
            flat = lambda v: v.rearrange("p c h -> p (c h)")
            act.activation(flat(e_all), bank[3][:, 0:NC * NH], ACT.Exp).then_inc(s_sumx, 1)
            act.activation(flat(dd_all), bank[4][:, 0:NC * NH], ACT.Exp).then_inc(s_sumx, 1)
            act.activation(flat(cd_all), bank[5][:, 0:NC * NH], ACT.Exp).then_inc(s_sumx, 1)
            act.wait_ge(s_pre, 1)
            act.wait_ge(s_fill, FILLS)

            def step(t, par):
                if on(t):
                    wait(act, q_table, t)
                    act.activation(touch, half_neg[:, 0:1], ACT.Exp).then_inc(q_table, 1)
                c, p = t, par
                if on(c):
                    wait(act, q_inx, c + 1)
                    wait(act, q_halo, c - 1)
                    for n in range(2):
                        act.copy(xbc[p][:, 3 * n:3 * n + 3, TAPS - 1:], bank[n][:, 0:3 * P]
                                 .rearrange("p (m t) -> p m t", m=3)).then_inc(q_xbe, 1)
                    wait(act, q_silx, c - 1)
                    for m in range(XT_TILES):
                        mm = act.activation(cv[p][:, m, :], bank[m // 3][:, (m % 3) * P:(m % 3 + 1) * P], ACT.Identity,
                                            bias=cb_sb[:, m:m + 1], scale=cw_sb[:, m, TAPS - 1:TAPS])
                    mm.then_inc(q_tap, 1)
                c, p = t - 1, 1 - par
                if on(c):
                    wait(act, q_seg, c + 1)
                    wait(act, q_y, c - 1)
                    for n in range(2):
                        mm = act.activation(em[p][:, 4 * n:4 * n + 4, :].rearrange("p h l -> p (h l)"), bank[5 + n][:, :],
                                            ACT.Exp)
                    mm.then_inc(q_exp, 1)
                c, p = t - 1, 1 - par
                if on(c):
                    wait(act, q_xt, c + 1)
                    wait(act, q_xdt, c - 1)
                    wait(act, q_xd, c - 1)
                    act.copy(x_sb[p].rearrange("p h d -> p (h d)"), bank[4][:, :]).then_inc(q_xte, 1)
                    wait(act, q_bc, c + 1)
                    wait(act, q_st, c - 1)
                    wait(act, q_cbm, c + 1)
                    act.copy(b_sb[p], bank[7][:, 0:P]).then_inc(q_be, 1)
                c, p = t - 1, 1 - par
                if on(c):
                    wait(act, q_inz, c + 1)
                    wait(act, q_yv, 4 * (c - 1))
                    act.activation(zs[p], bank[2][:, :], ACT.Silu).then_inc(q_silz, 1)
                c, p = t - 3, 1 - par
                if on(c):
                    wait(act, q_yv, 4 * c + 4)
                    wait(act, q_rms, 2 * (c - 1))
                    wait(act, q_sq, c)
                    act.activation(junk, y[p].rearrange("p h d -> p (h d)"), ACT.Square,
                                   accum_out=ssq[:, p:p + 1]).then_inc(q_sq, 1)
                if on(t + 1) or on(t - 5):
                    wait(act, q_ut, t + 2)
                    if on(t - 5):
                        wait(act, q_lg, t - 5)
                        mm = act.copy(x1T.rearrange("p k t -> p (k t)"), bank[0][:, D:2 * D])
                    if on(t + 1):
                        mm = act.copy(uT[1 - par].rearrange("p k t -> p (k t)"), bank[0][:, 0:D])
                    mm.then_inc(q_ute, 1)
                c, p = t - 3, 1 - par
                if on(c):
                    wait(act, q_yt, c + 1)
                    wait(act, q_op, c)
                    act.copy(yT.rearrange("p k t -> p (k t)"), bank[2][:, :]).then_inc(q_yte, 1)
                c, p = t, par
                if on(c):
                    wait(act, q_conv, CONV * c + CONV)
                    wait(act, q_y, c - 1)
                    act.activation(xs[p], cv[p], ACT.Silu).then_inc(q_silx, 1)

            mamba_steps(act, step, -1)

            act.wait_ge(s_rv, 2)
            act.activation(ex, lt, ACT.Exp).then_inc(s_rx, 1)
            act.wait_ge(s_route, 1)

            def bstep(i, r, held):
                ok = lambda k: not isinstance(k, int) or 0 <= k < BLOCKS
                if ok(i + 1):
                    c, p = i + 1, (r + 1) % 2
                    wait(act, g_xt, c + 1)
                    wait(act, g_w1, 2 * (c - 1))
                    act.copy(xgT[p].rearrange("p k t -> p (k t)"), bank[0][:, 0:D]).then_inc(g_xte, 1)
                if ok(i - 1):
                    c, p = i - 1, (r - 1) % 2
                    wait(act, g_ht, c + 1)
                    wait(act, g_w2, c)
                    for n in range(2):
                        act.copy(hT[:, 4 * n:4 * n + 4, :].rearrange("p k t -> p (k t)"), bank[3 + n][:, :]).then_inc(g_hte, 1)
                if ok(i):
                    c, p = i, r % 2
                    for n in range(2):
                        wait(act, g_hb, 2 * c + n + 1)
                        wait(act, g_ht, c - 1)
                        act.activation(h_sb[p][:, n * 512:(n + 1) * 512], hp[p][:, n * 512:(n + 1) * 512],
                                       ACT.Gelu).then_inc(g_h, 1)

            block_steps(act, bstep, -1, BLOCKS + 1)

        @block.vector
        def _(dve):
            dve.wait_ge(s_pre_dt, NC // 2)
            n = [0]

            def sp_step(ins):
                n[0] += 1
                ins.then_inc(s_sp, 1)
                dve.wait_ge(s_sp, n[0])

            psum_dt = bank[2][:, 0:NC * NH].rearrange("p (c h) -> p c h", h=NH)
            sp_step(dve.tensor_tensor(dtx, psum_dt, dtb_row.unsqueeze(1).broadcast_to([P, NC, NH]), ALU.add))
            sp_step(dve.scalar_tensor_tensor(out=dta, in0=dtx, scalar=-1.0, in1=dtx, op0=ALU.mult, op1=ALU.max))
            dve.wait_ge(s_spx, 1)
            sp_step(dve.tensor_scalar(dts, dta, 2.0, None, ALU.add))
            sp_step(dve.reciprocal(dts, dts))
            sp_step(dve.tensor_tensor(dts, dts, dta, ALU.mult))
            sp_step(dve.tensor_tensor(dtq, dts, dts, ALU.mult))
            sp_step(dve.tensor_scalar(dtp, dtq, 1.0 / 19, None, ALU.mult))
            for k in range(17, 1, -2):
                sp_step(dve.scalar_tensor_tensor(out=dtp, in0=dtp, scalar=1.0 / k, in1=dtq, op0=ALU.add, op1=ALU.mult))
            sp_step(dve.scalar_tensor_tensor(out=dtp, in0=dtp, scalar=1.0, in1=dts, op0=ALU.add, op1=ALU.mult))
            sp_step(dve.tensor_scalar(dtx, dtx, 0.0, None, ALU.max))
            sp_step(dve.scalar_tensor_tensor(out=dt_all, in0=dtp, scalar=2.0, in1=dtx, op0=ALU.mult, op1=ALU.add))
            dve.wait_ge(s_negA, 1)
            sp_step(dve.tensor_scalar(negA, negA, -1.0, None, ALU.mult))
            sp_step(dve.tensor_tensor(a_all, dt_all, negA.unsqueeze(1).broadcast_to([P, NC, NH]), ALU.mult))
            assert n[0] == SP_STEPS, n[0]
            dve.wait_ge(s_sumx, 2)
            dve.tensor_tensor(dd_all, dd_all, dt_all, ALU.mult).then_inc(s_pre, 1)
            dve.wait_ge(s_param2, 96)
            for k in range(KI):
                mm = dve.tensor_scalar(w_out[:, k, :], w_out[:, k, :], nw_col[:, k:k + 1], None, ALU.mult)
            mm.then_inc(s_wout, 1)
            dve.wait_ge(s_sumx, 3)
            dve.wait_ge(s_pre, 1)
            dve.wait_ge(s_fill, FILLS)

            def step(t, par):
                c, p = t - 1, 1 - par
                if on(c):
                    wait(dve, q_bc, c + 1)
                    dve.tensor_tensor(cbm[p], bank[7][:, P:2 * P], masks[:, M_LE, :], ALU.mult).then_inc(q_cbm, 1)
                c, p = t, par
                if on(c):
                    wait(dve, q_tap, c + 1)
                    for k in range(TAPS - 1):
                        for m in range(XT_TILES):
                            src = xbc[p][:, m, k:k + P]
                            if k and m == 0:
                                wait(dve, q_conv, CONV * c + XT_TILES * k)
                            dve.scalar_tensor_tensor(out=cv[p][:, m, :], in0=src, scalar=cw_sb[:, m, k:k + 1],
                                                     in1=cv[p][:, m, :], op0=ALU.mult, op1=ALU.add).then_inc(q_conv, 1)
                    wait(dve, q_conv, CONV * c + CONV)
                    dve.tensor_copy(xbc[p][:, :, 0:TAPS - 1], xbc[p][:, :, P:P + TAPS - 1]).then_inc(q_halo, 1)
                c, p = t - 1, 1 - par
                if on(c):
                    wait(dve, q_xte, c + 1)
                    wait(dve, q_y, c - 1)
                    dve.tensor_tensor(xdt[p], x_sb[p], heads(dt_all, c), ALU.mult).then_inc(q_xdt, 1)
                    wait(dve, q_exp, c + 1)
                    wait(dve, q_cbm, c + 1)
                    dve.tensor_tensor(em[p], em[p], cbm[p].unsqueeze(1).broadcast_to([P, NH, P]),
                                      ALU.mult).then_inc(q_m, 1)
                c, p = t - 2, par
                if on(c):
                    wait(dve, q_y, c + 1)
                    wait(dve, q_yt, c - 1)
                    wait(dve, q_sq, c - 1)
                    dve.tensor_tensor(y[p], bank[6][:, :].rearrange("p (h d) -> p h d", h=NH), heads(e_all, c),
                                      ALU.mult).then_inc(q_yv, 1)
                    wait(dve, q_yv, 4 * c + 1)
                    dve.tensor_tensor(y[p], bank[5][:, :].rearrange("p (h d) -> p h d", h=NH), y[p],
                                      ALU.add).then_inc(q_yv, 1)
                    wait(dve, q_yv, 4 * c + 2)
                    wait(dve, q_xd, c + 1)
                    dve.tensor_tensor(y[p], y[p], xD[p], ALU.add).then_inc(q_yv, 1)
                    wait(dve, q_yv, 4 * c + 3)
                    wait(dve, q_silz, c + 1)
                    dve.tensor_tensor(y[p].rearrange("p h d -> p (h d)"), y[p].rearrange("p h d -> p (h d)"), zs[p],
                                      ALU.mult).then_inc(q_yv, 1)
                    wait(dve, q_st, c + 1)
                    wait(dve, q_sd, c + 1)
                    dve.tensor_tensor(state[p], bank[4][:, :].rearrange("p (h d) -> p h d", h=NH), sdec[p],
                                      ALU.add).then_inc(q_s, 1)
                c, p = t - 4, par
                if on(c):
                    wait(dve, q_op, c + 1)
                    wait(dve, q_lg, c - 1)
                    wait(dve, q_rms, 2 * c + 2)
                    wait(dve, s_ures[p], 8 * (c - p) + 16)
                    dve.scalar_tensor_tensor(out=u_res[p], in0=bank[3][:, 0:D], scalar=rms[:, p:p + 1], in1=u_res[p],
                                             op0=ALU.mult, op1=ALU.add).then_inc(q_r, 1)
                c, p = t - 6, par
                if on(c):
                    wait(dve, q_lg, c + 1)
                    dve.tensor_copy(logits[:, bass.ds(c, 1), :].rearrange("p o e -> p (o e)"), bank[3][:, D:D + NE]
                                    ).then_inc(q_lge, 1)
                c, p = t - 4, par
                if on(c):
                    wait(dve, q_r, 3 * c + 1)
                    dve.bn_stats(bst[p], u_res[p]).then_inc(q_r, 1)
                    wait(dve, q_r, 3 * c + 2)
                    wait(dve, q_rstd, 2 * (c - 1))
                    settled(dve, s_dve_turns)
                    dve.bn_aggr(mv[p], bst[p]).then_inc(q_r, 1)
                    wait(dve, q_rstd, 2 * c + 2)
                    dve.tensor_scalar(u_res[p], u_res[p], mv[p][:, 0:1], rstd[:, p:p + 1], ALU.subtract,
                                      ALU.mult).then_inc(q_x1, 1)

            mamba_steps(dve, step, 0)

            dve.wait_ge(q_lge, NC)
            dve.wait_ge(q_x1, NC)
            r = [0]

            def rv(ins):
                r[0] += 1
                ins.then_inc(s_rv, 1)
                dve.wait_ge(s_rv, r[0])

            over_e = lambda v: v.unsqueeze(2).broadcast_to([P, NC, NE])
            mx, sm, prob, ms, pos, slot, blk, blk_id, tmp = (small[:, k, :] for k in range(9))
            tmp_i, slot_i, blk_i = (small[:, k, :].bitcast(I32) for k in range(9, 12))
            rv(dve.tensor_reduce(mx, logits, AX, ALU.max))
            rv(dve.tensor_tensor(lt, logits, over_e(mx), ALU.subtract))
            dve.wait_ge(s_rx, 1)
            rv(dve.tensor_reduce(sm, ex, AX, ALU.add))
            rv(dve.tensor_reduce(mx, ex, AX, ALU.max))
            rv(dve.tensor_tensor(lt, ex, over_e(mx), ALU.is_equal))
            rv(dve.tensor_tensor(lt, lt, prio.unsqueeze(1).broadcast_to([P, NC, NE]), ALU.mult))
            rv(dve.tensor_reduce(ms, lt, AX, ALU.max))
            rv(dve.tensor_tensor(onehot, lt, over_e(ms), ALU.is_equal))
            assert r[0] == ROUTE_ONEHOT
            rv(dve.reciprocal(prob, sm))
            dve.wait_ge(s_rp, 1)
            rv(dve.tensor_copy(pref[0].rearrange("p c e -> p (c e)"), bank[1][:, 0:NC * NE]))
            rv(dve.tensor_copy(ex.rearrange("p c e -> p (c e)"), bank[1][:, 0:NC * NE]))
            a, d = 0, 1
            while d < NC:
                rv(dve.tensor_copy(pref[1 - a][:, 0:d, :], pref[a][:, 0:d, :]))
                rv(dve.tensor_tensor(pref[1 - a][:, d:, :], pref[a][:, d:, :], pref[a][:, :NC - d, :], ALU.add))
                a, d = 1 - a, 2 * d
            blocks_i, blocks, end0, end1, start = (tiny[:, k, :] for k in range(5))
            rv(dve.tensor_scalar(blocks, pref[a][:, NC - 1, :], float(P - 1), None, ALU.add))
            rv(dve.tensor_copy(blocks_i.bitcast(I32), blocks))
            rv(dve.tensor_scalar(blocks_i.bitcast(I32), blocks_i.bitcast(I32), 7, None, ALU.logical_shift_right))
            rv(dve.tensor_copy(blocks, blocks_i.bitcast(I32)))
            rv(dve.tensor_copy(end0, blocks))
            ends, d = [end0, end1], 1
            while d < NE:
                rv(dve.tensor_copy(ends[1][:, 0:d], ends[0][:, 0:d]))
                rv(dve.tensor_tensor(ends[1][:, d:], ends[0][:, d:], ends[0][:, :NE - d], ALU.add))
                ends, d = ends[::-1], 2 * d
            end = ends[0]
            rv(dve.tensor_tensor(start, end, blocks, ALU.subtract))
            rv(dve.tensor_scalar(start, start, float(P), None, ALU.mult))
            rv(dve.tensor_tensor(lt, pref[a], ex, ALU.subtract))
            rv(dve.tensor_tensor(lt, lt, start.unsqueeze(1).broadcast_to([P, NC, NE]), ALU.add))
            rv(dve.tensor_tensor(lt.rearrange("p c e -> p (c e)"), bank[0][:, 0:NC * NE],
                                 lt.rearrange("p c e -> p (c e)"), ALU.add))
            rv(dve.tensor_tensor(lt, lt, onehot, ALU.mult))
            rv(dve.tensor_reduce(pos, lt, AX, ALU.add))
            rv(dve.tensor_copy(tmp_i, pos))
            rv(dve.tensor_scalar(slot_i, tmp_i, P - 1, None, ALU.bitwise_and))
            rv(dve.tensor_scalar(blk_i, tmp_i, 7, None, ALU.logical_shift_right))
            rv(dve.tensor_copy(slot, slot_i))
            rv(dve.tensor_copy(blk, blk_i))
            rv(dve.tensor_tensor(ge, iota_blk.unsqueeze(2).broadcast_to([P, BLOCKS, NE]),
                                 end.unsqueeze(1).broadcast_to([P, BLOCKS, NE]), ALU.is_ge))
            rv(dve.tensor_reduce(eb_f, ge, AX, ALU.add))
            rv(dve.tensor_scalar(eb_f, eb_f, float(NE - 1), None, ALU.min))
            rv(dve.tensor_copy(eb_i, eb_f))
            for g in range(NC // GT):
                if g:
                    dve.wait_ge(s_inv, g)
                sl = slice(GT * g, GT * g + GT)
                for k in range(GT):
                    ins = dve.tensor_scalar(oh_slot[:, k, :], iota_slot, slot[:, GT * g + k:GT * g + k + 1],
                                            None, ALU.is_equal)
                ins.then_inc(s_ohs, 1)
                for k in range(GT):
                    c = GT * g + k
                    ins = dve.tensor_scalar(oh_blk[:, 0, k, :], iota_blk, blk[:, c:c + 1], ids1[:, c:c + 1],
                                            ALU.is_equal, ALU.mult)
                ins.then_inc(s_ohs, 1)
                for k in range(GT):
                    c = GT * g + k
                    ins = dve.tensor_scalar(oh_blk[:, 1, k, :], iota_blk, blk[:, c:c + 1], prob[:, c:c + 1],
                                            ALU.is_equal, ALU.mult)
                ins.then_inc(s_ohs, 1)
            dve.wait_ge(s_inv, NC // GT)
            rv(dve.tensor_scalar(idx_z, bank[2][:, 0:BLOCKS], 0.0, float(T + 1), ALU.is_equal, ALU.mult))
            rv(dve.scalar_tensor_tensor(out=idx_f, in0=bank[2][:, 0:BLOCKS], scalar=-1.0, in1=idx_z,
                                        op0=ALU.add, op1=ALU.add))
            rv(dve.tensor_copy(prob_blk, bank[2][:, BLOCKS:2 * BLOCKS]))
            dve.tensor_copy(idx_i, idx_f).then_inc(s_route, 1)
            dve.wait_ge(s_route, 1)
            dve.wait_ge(s_late, 32 * LATE + 32)

            def experts(j):
                return [dve.value_load(eb_i[0:1, bass.ds(4 * j + r, 1)], min_val=0, max_val=NE - 1)
                        for r in range(-1, 4)]

            def bstep(i, r, held):
                ok = lambda k: not isinstance(k, int) or 0 <= k < BLOCKS

                def expert(k, n):
                    if held is not None:
                        return held[n + 1]
                    return dve.value_load(eb_i[0:1, k:k + 1], min_val=0, max_val=NE - 1)

                if ok(i):
                    c, p = i, r % 2
                    e = expert(c, r)
                    for n in range(2):
                        wait(dve, g_w1, 2 * c + n + 1)
                        wait(dve, g_h, 2 * (c - 1))
                        dve.tensor_tensor(hp[p][:, n * 512:(n + 1) * 512], bank[(1, 6)[p] + n][:, :],
                                          b1_rep[:, bass.ds(e, 1), n * 512:(n + 1) * 512].rearrange("p o f -> p (o f)"),
                                          ALU.add).then_inc(g_hb, 1)
                if ok(i - 1):
                    c, q, p = i - 1, (r - 1) % 4, (r - 1) % 2
                    wait(dve, g_w2, c + 1)
                    wait(dve, g_out[q], 4 * (c - q))
                    e = expert(c, r - 1)
                    dve.tensor_tensor(yo[q], bank[5][:, 0:D], b2_rep[:, bass.ds(e, 1), :].rearrange("p o d -> p (o d)"),
                                      ALU.add).then_inc(g_r, 1)
                    wait(dve, g_r, 4 * c + 1)
                    dve.scalar_tensor_tensor(out=yo[q], in0=yo[q], scalar=prob_blk[:, bass.ds(c, 1)], in1=xg[q],
                                             op0=ALU.mult, op1=ALU.add).then_inc(g_r, 1)
                    wait(dve, g_r, 4 * c + 2)
                    dve.bn_stats(st2[p], yo[q]).then_inc(g_r, 1)
                    wait(dve, g_r, 4 * c + 3)
                    wait(dve, g_rs, 2 * (c - 1))
                    settled(dve, s_dve_turns)
                    dve.bn_aggr(mv2[p], st2[p]).then_inc(g_r, 1)
                if ok(i - 1):
                    c, q, p = i - 1, (r - 1) % 4, (r - 1) % 2
                    wait(dve, g_rs, 2 * c + 2)
                    dve.tensor_scalar(yo[q], yo[q], mv2[p][:, 0:1], rstd2[p][:, 1:2], ALU.subtract,
                                      ALU.mult).then_inc(g_y, 1)

            block_steps(dve, bstep, 0, BLOCKS + 1, experts)


_INS = ["L0_attn_u", "L0_attn_in_proj_w", "L0_attn_conv_weight", "L0_attn_conv_bias", "L0_attn_dt_bias",
        "L0_attn_A_log", "L0_attn_D_param", "L0_attn_norm_weight", "L0_attn_out_proj_w",
        "L0_ffn_Wr", "L0_ffn_W1", "L0_ffn_b1", "L0_ffn_W2", "L0_ffn_b2"]


def kernel(**inputs):
    import concourse.bacc as bacc
    from concourse.bass_utils import run_bass_kernel_spmd as run

    nc = bacc.Bacc("TRN2", target_bir_lowering=False, num_devices=1)
    arrays, args = {}, []
    channels = lambda a: a.reshape(a.shape[0] // P, P, -1).swapaxes(0, 1)
    for name in _INS:
        a = np.asarray(inputs[name])
        if name.endswith("conv_weight"):
            a = channels(a)
        elif name.endswith(("conv_bias", "norm_weight")):
            a = channels(a)[:, :, 0]
        a = np.ascontiguousarray(a)
        arrays[f"in_{name}"] = a
        args.append(nc.dram_tensor(f"in_{name}", a.shape, mybir.dt.from_np(a.dtype), kind="ExternalInput").ap())
    arrays["in_constants"] = constants()
    args.append(nc.dram_tensor("in_constants", (P, CW), F32, kind="ExternalInput").ap())
    out = nc.dram_tensor("out", (T, D), F32, kind="ExternalOutput").ap()
    build(nc, *args, out)
    r = run(nc, [arrays], core_ids=[0])
    return r.results[0]["out"].reshape(NB, L, D)
```

```python
from contextlib import ExitStack

import numpy as np

import concourse.bass as bass
from concourse import mybir

ALU = mybir.AluOpType
ACT = mybir.ActivationFunctionType
AX = mybir.AxisListType.X
F32 = mybir.dt.float32
I32 = mybir.dt.int32
F32R = mybir.dt.float32r
HI_BITS = -(1 << 12)

P = 128
NB, L, D = 2, 2048, 256
DI, NS, NH, HD = 512, 128, 8, 64
TAPS = 4
NPROJ = 2 * DI + 2 * NS + NH
XT_TILES = (DI + 2 * NS) // P
XD_TILES = DI // P
NE, FF = 8, 1024
EPS = 1e-5
T = NB * L
NC = T // P
BLOCKS = T // P + NE - 1
COLS = BLOCKS + BLOCKS % 2
LATE = 3
KD, KF, KI = D // P, FF // P, DI // P

M_ID, M_LE, M_GT, M_LT = range(4)
N_MASKS = 4
CW = N_MASKS * P + COLS + NE + NC + P
ARENA = 48200
FILLS = 7
CONV = (TAPS - 1) * XT_TILES
SP_STEPS = 19
PARTS = [(0, NC - 6 * NB), (NC - 6 * NB, NC)]
ROUTE_ONEHOT = 8


def constants():
    k, m = np.arange(P)[:, None], np.arange(P)[None, :]
    masks = [k == m, k <= m, k > m, k < m]
    c, rest = np.zeros((P, CW), np.float32), N_MASKS * P
    for n, mask in enumerate(masks):
        c[:, n * P:(n + 1) * P] = mask
    c[:, rest:rest + COLS] = np.arange(COLS)
    c[:, rest + COLS:rest + COLS + NE] = NE - np.arange(NE)
    chunk = np.arange(NC)
    c[:, rest + COLS + NE:CW - P] = (chunk % NB) * L + (chunk // NB) * P + k + 1
    c[:, CW - P:] = np.arange(P)
    return c


def wait(eng, sem, n):
    if not isinstance(n, int) or n > 0:
        eng.wait_ge(sem, n)


def settled(eng, turns):
    eng.sem_inc(turns, 1)


def edge(eng, sem, c, n):
    if isinstance(c, int):
        wait(eng, sem, n)


def on(c):
    return not isinstance(c, int) or 0 <= c < NC


def mamba_steps(eng, step, first):
    peeled, lag = 8, 6
    for t in range(first, peeled):
        step(t, t % 2)
    with eng.Fori(peeled // 2, NC // 2 - 1) as j:
        for par in range(2):
            step(2 * j + par, par)
    for t in range(NC - 2, NC + lag):
        step(t, t % 2)


def pre_steps(eng, pair_step, part_step):
    pairs = NC // NB
    for pair in range(4):
        pair_step(pair, pair, 0)
    with eng.Fori(1, pairs // 4 - 1) as q:
        for r in range(4):
            pair_step(4 * q + r, r, 0)
    part_step(0)
    for pair in range(pairs - 4, pairs):
        pair_step(pair, pair % 4, 1)
    part_step(1)


def block_steps(eng, step, first, last, before=None):
    for i in range(first, 8):
        step(i, i % 4, None)
    tail = (BLOCKS - 2) // 4 * 4
    with eng.Fori(2, tail // 4) as j:
        held = before(j) if before else None
        for r in range(4):
            step(4 * j + r, r, held)
    for i in range(tail, last):
        step(i, i % 4, None)


def build(nc, u, in_proj_w, conv_w, conv_b, dt_bias, a_log, d_param, norm_w, out_proj_w,
          wr, w1, b1, w2, b2, consts, out):
    x1_rows = nc.dram_tensor("x1_rows", [T + 1, D], F32, kind="Internal").ap()
    ctx = ExitStack()
    with ctx:
        wsize = KD * FF + KF * D
        wtotal = NE * wsize
        arena = ctx.enter_context(nc.sbuf_tensor("arena", [P, ARENA], F32))
        GT = 4
        values = 3
        one_pass = ctx.enter_context(nc.sbuf_tensor("one_pass", [P, P + max(2 * NH * P, 2 * GT * P + values * NC * COLS)],
                                                    F32R))
        ub = [one_pass[:, n * NH * P:(n + 1) * NH * P].rearrange("p (h l) -> p h l", h=NH) for n in range(2)]
        mask_gt = one_pass[:, one_pass.shape[1] - P:]
        oh_slot = [one_pass[:, n * GT * P:(n + 1) * GT * P].rearrange("p (g s) -> p g s", g=GT) for n in range(2)]
        oh_blk = (one_pass[:, 2 * GT * P:2 * GT * P + values * NC * COLS]
                  .rearrange("p (v c b) -> p v c b", v=values, c=NC))
        at = [0]

        def carve(*shape):
            n = int(np.prod(shape))
            v = arena[:, at[0]:at[0] + n]
            at[0] += n
            if len(shape) == 2:
                v = v.rearrange("p (a b) -> p a b", a=shape[0])
            elif len(shape) == 3:
                v = v.rearrange("p (a b c) -> p a b c", a=shape[0], b=shape[1])
            return v

        w1_sb = arena[:, 0:NE * KD * FF].rearrange("p (e k f) -> p e k f", e=NE, k=KD)
        w2_sb = arena[:, NE * KD * FF:wtotal].rearrange("p (e k d) -> p e k d", e=NE, k=KF)
        at[0] = wtotal
        cst = carve(CW)
        masks = cst[:, 0:N_MASKS * P].rearrange("p (n m) -> p n m", n=N_MASKS)
        ident = masks[:, M_ID, :]
        iota_blk = cst[:, N_MASKS * P:N_MASKS * P + COLS]
        prio = cst[:, N_MASKS * P + COLS:N_MASKS * P + COLS + NE]
        ids1 = cst[:, N_MASKS * P + COLS + NE:CW - P]
        iota_slot = cst[:, CW - P:CW]
        ones = carve(P)
        half_neg = carve(2)
        gelu_touch = carve(1)
        logits = carve(NC, NE)
        wr_sb = carve(KD, NE)
        zrow = carve(D)
        persistent_end = at[0]

        b1_col = carve(NE, KF)
        b2_rep = carve(NE, D)
        idx_f = carve(COLS)
        idx_z = carve(COLS)
        idx_i = carve(COLS).bitcast(I32)
        prob_blk = carve(COLS)
        eb_f = carve(COLS)
        eb_i = carve(COLS).bitcast(I32)
        idx_col = [carve(1).bitcast(I32) for _ in range(4)]
        idx_out = [carve(1).bitcast(I32) for _ in range(4)]
        temp_start = at[0]
        xg = [carve(D) for _ in range(4)]
        yo = [carve(D) for _ in range(4)]
        xgT = [carve(KD, P) for _ in range(2)]
        w1_cur = [carve(KD, FF) for _ in range(2)]
        b1_cur = [carve(KF) for _ in range(2)]
        hT = [carve(KF, P) for _ in range(2)]
        st2 = [carve(6) for _ in range(2)]
        mv2 = [carve(2) for _ in range(2)]
        rstd2 = [carve(2) for _ in range(2)]
        assert at[0] <= ARENA
        at[0] = temp_start
        lt = carve(NC, NE)
        ex = carve(NC, NE)
        onehot = carve(NC, NE)
        pref = [carve(NC // 2 + NC, NE) for _ in range(2)]
        ends = [carve(NE // 2 + NE) for _ in range(2)]
        small = carve(16, NC)
        PROB_HI = 7
        blk_eq = carve(NC, COLS)
        ge = carve(COLS, NE)
        tiny = carve(16, NE)
        assert at[0] <= ARENA, at[0]

        at[0] = persistent_end
        w_in = carve(KD, NPROJ)
        w_out = carve(KI, D)
        nw_col = carve(KI)
        cw_sb = carve(XT_TILES, TAPS)
        cb_sb = carve(XT_TILES)
        d_row = carve(NH)
        dtb_row = carve(NH)
        negA = carve(NH)
        a_all = carve(NC, NH)
        dt_all = carve(NC, NH)
        e_all = carve(NC, NH)
        cd_all = carve(NC, NH)
        dd_all = carve(NC, NH)
        u_in = [carve(D) for _ in range(2)]
        uT = [carve(KD, P) for _ in range(2)]
        xs = [carve(XT_TILES, P) for _ in range(2)]
        xdt = [carve(NH, HD) for _ in range(2)]
        state = [carve(NH, HD) for _ in range(2)]
        sdec = [carve(NH, HD) for _ in range(2)]
        y = [carve(NH, HD) for _ in range(2)]
        yT = carve(KI, P)
        x1T = carve(KD, P)
        cbm = [carve(P) for _ in range(2)]
        b_sb = [carve(P) for _ in range(2)]
        ssq = carve(2)
        rms = carve(2)
        bst = [carve(6) for _ in range(2)]
        mv = [carve(2) for _ in range(2)]
        rstd = carve(2)
        u_res = [carve(D) for _ in range(2)]
        assert at[0] <= ARENA, at[0]
        at[0] = NE * KD * FF + (NE - LATE) * KF * D
        xbc = [carve(XT_TILES, TAPS - 1 + P) for _ in range(2)]
        cv = [carve(XT_TILES, P) for _ in range(2)]
        x_sb = [carve(NH, HD) for _ in range(2)]
        xdd = [carve(NH, HD) for _ in range(2)]
        a_hi = carve(NC, NH)
        a_lo = carve(NC, NH)
        assert at[0] <= wtotal, (at[0], wtotal)
        at[0] = (NE - LATE) * KD * FF
        em = [carve(NH, P) for _ in range(2)]
        junk = carve(DI)
        touch = carve(1)
        xD = [carve(NH, HD) for _ in range(2)]
        zs = [carve(DI) for _ in range(2)]
        assert at[0] <= NE * KD * FF
        at[0] = (NE - LATE) * KD * FF
        pre_u = [carve(NB, D) for _ in range(4)]
        pre_uT = [carve(NB * KD, P) for _ in range(2)]
        pre_dtT = [carve(NB * P) for _ in range(2)]
        dtx = carve(NC, NH)
        dta = carve(NC, NH)
        dts = carve(NC, NH)
        dtq = carve(NC, NH)
        dtp = carve(NC, NH)
        assert at[0] <= NE * KD * FF

        bank = [ctx.enter_context(nc.psum_tensor(f"bank{n}", [P, 512], F32)) for n in range(8)]

        def sem(name):
            return ctx.enter_context(nc.semaphore(name))

        s_const = sem("const_loaded")
        s_param = sem("dt_params_loaded")
        s_param2 = sem("mamba_params_loaded")
        s_early = sem("early_experts_loaded")
        s_late = sem("late_experts_loaded")
        s_zrow = sem("zero_row_stored")
        s_fill = sem("fills_done")
        s_pool_turns, s_dve_turns, s_sp_turns = sem("pool_turns"), sem("dve_turns"), sem("sp_turns")
        s_wout = sem("out_proj_scaled")
        s_pre_u = [sem(f"pre_u_loaded{n}") for n in range(4)]
        s_pre_t = sem("pre_transposed")
        s_pre_ev = sem("pre_uT_ready")
        s_pre_p, s_pre_pe = sem("pre_dt_product"), sem("pre_dt_copied")
        s_pre_dt = sem("pre_dt_transposed")
        s_negA = sem("negA_steps")
        s_sp = sem("softplus_steps")
        s_split = sem("a_split")
        s_spx = sem("softplus_exp")
        s_sums = sem("chunk_sums")
        s_sumx = sem("chunk_sums_exp")
        s_pre = sem("dt_phase_done")
        s_uin = [sem(f"u_in_loaded{n}") for n in range(2)]
        s_ures = [sem(f"u_res_loaded{n}") for n in range(2)]
        s_x1st = [sem(f"x1_stored{n}") for n in range(2)]
        q_table = sem("table_touched")
        q_ut, q_ute = sem("u_and_x1_transposed"), sem("uT_and_x1T_ready")
        q_inx, q_xbe, q_tap, q_halo = sem("xbc_product"), sem("xbc_ready"), sem("last_tap_ready"), sem("halo_copied")
        q_conv, q_silx = sem("conv_steps"), sem("xs_ready")
        q_inz, q_silz = sem("z_product"), sem("zs_ready")
        q_xt, q_xte = sem("x_transposed"), sem("x_ready")
        q_bc, q_be, q_cbm = sem("b_and_cb"), sem("b_ready"), sem("cb_masked")
        q_ub, q_seg, q_exp, q_m = sem("a_mask_ready"), sem("segment_sums"), sem("decay_ready"), sem("m_ready")
        q_xdt, q_xdd, q_xd = sem("xdt_ready"), sem("xdd_ready"), sem("xD_ready")
        q_y, q_yv, q_sq = sem("y_products"), sem("y_steps"), sem("y_squared")
        q_st, q_sd, q_s = sem("state_product"), sem("state_decayed"), sem("state_updated")
        q_rms, q_yt, q_yte = sem("rms_steps"), sem("y_transposed"), sem("yT_ready")
        q_op, q_r, q_rstd, q_x1 = sem("out_product"), sem("residual_steps"), sem("rstd_steps"), sem("x1_ready")
        q_lg, q_lge = sem("logit_product"), sem("logits_ready")
        s_ohe, s_ohb = sem("block_onehots_ready"), sem("block_values_ready")
        s_rv, s_rx, s_rp, s_ohs, s_inv = (sem("route_steps"), sem("route_exp"), sem("route_products"),
                                          sem("onehots_ready"), sem("slots_product"))
        s_route = sem("routing_done")
        g_idx, g_x = sem("gather_index_ready"), [sem(f"rows_gathered{n}") for n in range(4)]
        g_xt, g_xte = sem("xg_transposed"), sem("xgT_ready")
        g_cur, g_w1, g_h, g_w2 = sem("w1_and_b1_fetched"), sem("w1_product"), sem("hT_ready"), sem("w2_product")
        g_r, g_rs, g_y = sem("block_residual_steps"), sem("block_rstd_steps"), sem("block_rows_ready")
        g_oidx, g_out = sem("scatter_index_ready"), [sem(f"rows_scattered{n}") for n in range(4)]

        def chunk_rows(c, par):
            return (c - par) * (P // 2) + par * L

        def heads(all_chunks, c, n=HD):
            return (all_chunks[:, bass.ds(c, 1), :].rearrange("p o h -> p (o h)").unsqueeze(2)
                    .broadcast_to([P, NH, n]))

        block = ctx.enter_context(nc.Block())

        @block.sync
        def _(sp):
            in_proj = in_proj_w.rearrange("(k p) n -> p k n", p=P)
            sp.dma_start(w_in[:, :, NPROJ - NH:], in_proj[:, :, NPROJ - NH:]).then_inc(s_param, 16)
            sp.dma_start(cst, consts).then_inc(s_const, 16)
            sp.dma_start(dtb_row, dt_bias.partition_broadcast(P)).then_inc(s_param, 16)
            sp.dma_start(negA, a_log.partition_broadcast(P)).then_inc(s_param, 16)

            def load_pair(pair, r, part):
                wait(sp, s_pre_t, pair - 3)
                sp.dma_start(pre_u[r], u[:, bass.ds(pair * P, P), :].rearrange("b p d -> p b d")).then_inc(s_pre_u[r], 16)

            pre_steps(sp, load_pair, lambda part: None)
            sp.dma_start(w_in[:, :, 0:NPROJ - NH], in_proj[:, :, 0:NPROJ - NH]).then_inc(s_param2, 16)
            sp.dma_start(w_out[:, :, :], out_proj_w.rearrange("(k p) n -> p k n", p=P)).then_inc(s_param2, 16)
            sp.dma_start(nw_col, norm_w).then_inc(s_param2, 16)
            sp.dma_start(cw_sb[:, :, :], conv_w).then_inc(s_param2, 16)
            sp.dma_start(cb_sb, conv_b).then_inc(s_param2, 16)
            sp.dma_start(d_row, d_param.partition_broadcast(P)).then_inc(s_param2, 16)
            sp.dma_start(wr_sb[:, :, :], wr.rearrange("(k p) e -> p k e", p=P)).then_inc(s_param2, 16)
            sp.wait_ge(s_fill, 1)
            sp.dma_start(x1_rows[T:T + 1, :], zrow[0:1, :]).then_inc(s_zrow, 16)

            def step(t, par):
                if on(t - 5):
                    wait(sp, q_x1, t - 4)
                    settled(sp, s_sp_turns)
                    sp.dma_start(x1_rows[bass.ds(chunk_rows(t - 5, 1 - par), P), :], u_res[1 - par]
                                 ).then_inc(s_x1st[1 - par], 16)
                if on(t + 2):
                    wait(sp, q_ut, t + 1)
                    c = t + 2
                    sp.dma_start(u_in[par], u[par, bass.ds((c - par) * (P // 2), P), :]).then_inc(s_uin[par], 16)
                c, p = t - 3, 1 - par
                if on(c):
                    if not isinstance(t, int) or t >= 5:
                        wait(sp, q_ut, t + 2)
                    wait(sp, s_x1st[p], 8 * (c - 2 - p) + 16)
                    settled(sp, s_sp_turns)
                    sp.dma_start(u_res[p], u[p, bass.ds((c - p) * (P // 2), P), :]).then_inc(s_ures[p], 16)

            mamba_steps(sp, step, -2)

            sp.wait_ge(q_lge, NC)
            sp.wait_ge(q_s, NC)
            sp.wait_ge(q_x1, NC)
            sp.wait_ge(q_sq, NC)
            for par in range(2):
                sp.wait_ge(s_x1st[par], 16 * NC // 2)
            sp.dma_start(b1_col[:, :, :].rearrange("p e k -> p (e k)"), b1).then_inc(s_late, 16)
            sp.dma_start(b2_rep[:, :, :].rearrange("p e f -> p (e f)"),
                         b2.rearrange("e f -> (e f)").partition_broadcast(P)).then_inc(s_late, 16)

        @block.gpsimd
        def _(pool):
            pool.memset(zrow, 0.0).then_inc(s_fill, 1)
            pool.memset(ones, 1.0).then_inc(s_fill, 1)
            pool.memset(half_neg, -0.5).then_inc(s_fill, 1)
            pool.memset(state[0][:, :, :], 0.0).then_inc(s_fill, 1)
            pool.memset(state[1][:, :, :], 0.0).then_inc(s_fill, 1)
            for par in range(2):
                pool.memset(xbc[par][:, :, 0:TAPS - 1], 0.0).then_inc(s_fill, 1)
            pool.wait_ge(s_fill, FILLS)
            pool.wait_ge(s_param2, 112)
            pool.wait_ge(s_pre, 1)
            pool.wait_ge(s_sumx, 3)
            pool.wait_ge(s_split, 3)
            pool.wait_ge(s_sp, 1 + 2 * SP_STEPS)

            def step(t, par):
                c, p = t - 1, 1 - par
                if on(c):
                    wait(pool, q_xte, c + 1)
                    wait(pool, q_st, c - 1)
                    pool.tensor_tensor(xdd[p], x_sb[p], heads(dd_all, c), ALU.mult).then_inc(q_xdd, 1)
                    wait(pool, q_yv, 4 * (c - 1))
                    pool.tensor_tensor(xD[p], x_sb[p], d_row.unsqueeze(2).broadcast_to([P, NH, HD]),
                                       ALU.mult).then_inc(q_xd, 1)
                c, p = t, par
                if on(c):
                    wait(pool, q_seg, c)
                    for part, values in enumerate((a_hi, a_lo)):
                        pool.tensor_tensor(ub[part], heads(values, c, P), masks[:, M_LE, :].unsqueeze(1)
                                           .broadcast_to([P, NH, P]), ALU.mult).then_inc(q_ub, 1)
                c, p = t - 2, par
                if on(c):
                    wait(pool, q_s, c - 1)
                    pool.tensor_tensor(sdec[p], state[p], heads(cd_all, c), ALU.mult).then_inc(q_sd, 1)
                c, p = t - 3, 1 - par
                if on(c):
                    wait(pool, q_sq, c + 1)
                    wait(pool, q_r, 3 * (c - 2) + 1)
                    settled(pool, s_pool_turns)
                    pool.tensor_scalar(rms[:, p:p + 1], ssq[:, p:p + 1], 1.0 / DI, EPS, ALU.mult, ALU.add
                                       ).then_inc(q_rms, 1)
                    wait(pool, q_rms, 2 * c + 1)
                    pool.tensor_tensor(rms[:, p:p + 1], rms[:, p:p + 1], half_neg[:, 0:1], ALU.pow).then_inc(q_rms, 1)
                c, p = t - 4, par
                if on(c):
                    wait(pool, q_r, 3 * c + 3)
                    wait(pool, q_x1, c - 1)
                    settled(pool, s_pool_turns)
                    pool.tensor_scalar(rstd[:, p:p + 1], mv[p][:, 1:2], EPS, None, ALU.add).then_inc(q_rstd, 1)
                    wait(pool, q_rstd, 2 * c + 1)
                    pool.tensor_tensor(rstd[:, p:p + 1], rstd[:, p:p + 1], half_neg[:, 0:1], ALU.pow
                                       ).then_inc(q_rstd, 1)

            mamba_steps(pool, step, 0)

            for g in range(NC // GT):
                pool.wait_ge(s_ohe, g + 1)
                cs = slice(g * GT, g * GT + GT)
                for v, value in enumerate((ids1, small[:, PROB_HI, :])):
                    pool.tensor_tensor(oh_blk[:, v, cs, :], blk_eq[:, cs, :],
                                       value[:, cs].unsqueeze(2).broadcast_to([P, GT, COLS]), ALU.mult
                                       ).then_inc(s_ohb, 1)

            pool.wait_ge(s_route, 1)
            pool.wait_ge(s_zrow, 16)
            for par in range(2):
                pool.wait_ge(s_x1st[par], 16 * NC // 2)
            limit_in, limit_out = T, T - 1

            def bstep(i, r, held):
                ok = lambda k: not isinstance(k, int) or 0 <= k < BLOCKS
                if ok(i + 2):
                    c, q = i + 2, (r + 2) % 4
                    wait(pool, g_y, c - 3)
                    pool.tensor_copy(idx_col[q], idx_i[:, bass.ds(c, 1)]).then_inc(g_idx, 1)
                    wait(pool, g_idx, c + 1)
                    settled(pool, s_pool_turns)
                    pool.indirect_dma_start(xg[q], None, x1_rows[:, :],
                                            bass.IndirectOffsetOnAxis(ap=idx_col[q], axis=0),
                                            bounds_check=limit_in, oob_is_err=False).then_inc(g_x[q], 16)
                if ok(i - 3):
                    c, q = i - 3, (r - 3) % 4
                    wait(pool, g_out[q], 4 * (c - q))
                    pool.tensor_copy(idx_out[q], idx_i[:, bass.ds(c, 1)]).then_inc(g_oidx, 1)
                    wait(pool, g_oidx, c + 1)
                    wait(pool, g_y, c + 1)
                    settled(pool, s_pool_turns)
                    pool.indirect_dma_start(out, bass.IndirectOffsetOnAxis(ap=idx_out[q], axis=0), yo[q], None,
                                            bounds_check=limit_out, oob_is_err=False).then_inc(g_out[q], 16)
                if ok(i - 1):
                    c, q = i - 1, (r - 1) % 4
                    p = (r - 1) % 2
                    wait(pool, g_r, 4 * c + 4)
                    wait(pool, g_y, c - 1)
                    settled(pool, s_pool_turns)
                    pool.tensor_scalar(rstd2[p][:, 0:1], mv2[p][:, 1:2], EPS, None, ALU.add).then_inc(g_rs, 1)
                    wait(pool, g_rs, 2 * c + 1)
                    pool.tensor_tensor(rstd2[p][:, 1:2], rstd2[p][:, 0:1], half_neg[:, 0:1], ALU.pow
                                       ).then_inc(g_rs, 1)

            block_steps(pool, bstep, -2, BLOCKS + 3)
            for q in range(4):
                pool.wait_ge(g_out[q], 16 * len(range(q, BLOCKS, 4)))

        @block.tensor
        def _(pe):
            pe.wait_ge(s_const, 16)
            pe.wait_ge(s_param, 48)

            def transposes(pair, r):
                pe.wait_ge(s_pre_u[r], 4 * (pair - r) + 16)
                wait(pe, s_pre_ev, pair - 1)
                for b in range(NB):
                    for k in range(KD):
                        mm = pe.transpose(bank[r % 2][:, (b * KD + k) * P:(b * KD + k + 1) * P],
                                          pre_u[r][:, b, k * P:(k + 1) * P], ident)
                mm.then_inc(s_pre_t, 1)

            def products(pair, r):
                pe.wait_ge(s_pre_ev, pair + 1)
                wait(pe, s_pre_pe, pair - 1)
                by_k = pre_uT[r % 2].rearrange("p (b k) t -> p k b t", b=NB)
                for k in range(KD):
                    mm = pe.matmul(bank[3 + r % 2][0:NH, 0:NB * P], w_in[:, k, NPROJ - NH:NPROJ], by_k[:, k, :, :],
                                   start=(k == 0), stop=(k == KD - 1))
                mm.then_inc(s_pre_p, 1)

            def back(pair, r, part):
                pe.wait_ge(s_pre_pe, pair + 1)
                for b in range(NB):
                    mm = pe.matmul(bank[(2, 6)[part]][:, bass.ds(pair * (NB * NH) + b * NH, NH)],
                                   pre_dtT[r % 2][0:NH, b * P:(b + 1) * P], ident[0:NH, 0:NH], start=True, stop=True)
                mm.then_inc(s_pre_dt, 1)

            def pre_pair(pair, r, part):
                transposes(pair, r)
                if not isinstance(pair, int) or pair > 0:
                    products(pair - 1, (r - 1) % 4)
                if not isinstance(pair, int) or pair > 1:
                    back(pair - 2, (r - 2) % 4, part)

            def pre_part(part):
                if part == 1:
                    products(NC // NB - 1, 3)
                    back(NC // NB - 2, 2, part)
                    back(NC // NB - 1, 3, part)

            pre_steps(pe, pre_pair, pre_part)

            def turn(c, behind):
                return min(c + behind, NC) if isinstance(c, int) else c + behind

            def u_and_x1(t, par):
                if on(t + 1) or on(t - 5):
                    edge(pe, q_ute, t, t + 1)
                    if on(t):
                        wait(pe, q_tap, t + 1)
                    if on(t + 1):
                        wait(pe, s_uin[1 - par], 8 * (t + par) + 16)
                        for k in range(KD):
                            mm = pe.transpose(bank[0][:, k * P:(k + 1) * P], u_in[1 - par][:, k * P:(k + 1) * P], ident)
                    if on(t - 5):
                        wait(pe, q_x1, t - 4)
                        for k in range(KD):
                            mm = pe.transpose(bank[0][:, D + k * P:D + (k + 1) * P], u_res[1 - par][:, k * P:(k + 1) * P],
                                              ident)
                    mm.then_inc(q_ut, 1)

            def channels(t, par):
                c, p = t, par
                if on(c):
                    wait(pe, q_ute, c + 1)
                    wait(pe, q_tap, c)
                    for m in range(XT_TILES):
                        lo = DI + m * P
                        for k in range(KD):
                            mm = pe.matmul(bank[m // 3][:, (m % 3) * P:(m % 3 + 1) * P], w_in[:, k, lo:lo + P],
                                           uT[p][:, k, :], start=(k == 0), stop=(k == KD - 1))
                    mm.then_inc(q_inx, 1)

            pe.wait_ge(s_param2, 112)
            pe.wait_ge(s_pre_ev, NC // NB)
            u_and_x1(-1, 1)
            channels(0, 0)
            pe.wait_ge(s_sp, 1 + 2 * SP_STEPS)
            flat = lambda v: v.rearrange("p c h -> p (c h)")
            pe.wait_ge(s_fill, FILLS)
            pe.matmul(bank[3][:, 0:NC * NH], masks[:, M_LE, :], flat(a_all), start=True, stop=True)
            pe.matmul(bank[4][:, 0:NC * NH], masks[:, M_GT, :], flat(a_all), start=True, stop=True)
            pe.matmul(bank[5][:, 0:NC * NH], ones, flat(a_all), start=True, stop=True).then_inc(s_sums, 1)
            pe.wait_ge(s_pre, 1)
            pe.wait_ge(s_sumx, 3)
            pe.wait_ge(s_param2, 112)
            pe.wait_ge(s_wout, 1)

            def out_and_logits(t, par):
                c, p = t - 4, par
                if on(c):
                    wait(pe, q_yte, c + 1)
                    wait(pe, q_r, 3 * (c - 1) + 1)
                    wait(pe, q_lge, c - 2)
                    for k in range(KI):
                        mm = pe.matmul(bank[3][:, 0:D], yT[:, k, :], w_out[:, k, :], start=(k == 0), stop=(k == KI - 1))
                    mm.then_inc(q_op, 1)
                c, p = t - 6, par
                if on(c):
                    wait(pe, q_ute, t + 1)
                    edge(pe, q_lge, c, c)
                    if isinstance(t, int):
                        wait(pe, q_r, 3 * min(t - 5, NC - 1) + 1)
                    for k in range(KD):
                        mm = pe.matmul(bank[3][:, D:D + NE], x1T[:, k, :], wr_sb[:, k, :], start=(k == 0), stop=(k == KD - 1))
                    mm.then_inc(q_lg, 1)

            def y_products(t, par):
                c, p = t - 2, par
                if on(c):
                    wait(pe, q_m, c + 1)
                    wait(pe, q_xdt, c + 1)
                    wait(pe, q_exp, turn(c, 2))
                    edge(pe, q_yv, c, 4 * (c - 1) + 2)
                    for h in range(NH):
                        pe.matmul(bank[5][:, h * HD:(h + 1) * HD], em[p][:, h, :], xdt[p][:, h, :], start=True, stop=True)
                    wait(pe, q_s, c - 1)
                    pe.matmul(bank[6][:, :], xs[p][:, XD_TILES + 1, :], state[p].rearrange("p h d -> p (h d)"),
                              start=True, stop=True).then_inc(q_y, 1)

            def step(t, par):
                if not isinstance(t, int) or t > 0:
                    channels(t, par)
                c, p = t - 1, 1 - par
                if on(c):
                    wait(pe, q_ub, 2 * c + 2)
                    wait(pe, q_yv, 4 * (c - 2) + 2)
                    edge(pe, q_exp, c, c)
                    for n in range(2):
                        for part in range(2):
                            mm = pe.matmul(bank[5 + n][:, :], mask_gt,
                                           ub[part][:, 4 * n:4 * n + 4, :].rearrange("p h l -> p (h l)"),
                                           start=(part == 0), stop=(part == 1))
                    mm.then_inc(q_seg, 1)
                    wait(pe, q_yte, c - 2)
                    edge(pe, q_silz, c, c)
                    for k in range(KD):
                        mm = pe.matmul(bank[2][:, :], uT[p][:, k, :], w_in[:, k, 0:DI], start=(k == 0), stop=(k == KD - 1))
                    mm.then_inc(q_inz, 1)
                    wait(pe, q_silx, c + 1)
                    wait(pe, q_s, c - 1)
                    edge(pe, q_xte, c, c)
                    for m in range(XD_TILES):
                        mm = pe.transpose(bank[4][:, m * P:(m + 1) * P], xs[p][:, m, :], ident)
                    mm.then_inc(q_xt, 1)
                    wait(pe, q_be, c)
                    wait(pe, q_cbm, c)
                    pe.transpose(bank[7][:, 0:P], xs[p][:, XD_TILES, :], ident)
                    pe.matmul(bank[7][:, P:2 * P], xs[p][:, XD_TILES, :], xs[p][:, XD_TILES + 1, :],
                              start=True, stop=True).then_inc(q_bc, 1)
                order = (u_and_x1, out_and_logits, y_products)
                for stage in order if on(t) else order[::-1][:2]:
                    stage(t, par)
                c, p = t - 3, 1 - par
                if on(c):
                    wait(pe, q_yv, 4 * c + 4)
                    wait(pe, q_silz, turn(c, 3))
                    edge(pe, q_yte, c, c)
                    yf = y[p].rearrange("p h d -> p (h d)")
                    for k in range(KI):
                        mm = pe.transpose(bank[2][:, k * P:(k + 1) * P], yf[:, k * P:(k + 1) * P], ident)
                    mm.then_inc(q_yt, 1)
                c, p = t - 2, par
                if on(c):
                    wait(pe, q_xdd, c + 1)
                    wait(pe, q_be, c + 1)
                    wait(pe, q_xte, turn(c, 2))
                    edge(pe, q_s, c, c)
                    pe.matmul(bank[4][:, :], b_sb[p], xdd[p].rearrange("p h d -> p (h d)"),
                              start=True, stop=True).then_inc(q_st, 1)
                if not on(t):
                    u_and_x1(t, par)

            mamba_steps(pe, step, 0)

            pe.wait_ge(s_rv, ROUTE_ONEHOT)
            pe.wait_ge(q_lge, NC)
            pe.matmul(bank[0][:, 0:NC * NE], masks[:, M_LT, :], flat(onehot), start=True, stop=True)
            pe.matmul(bank[1][:, 0:NC * NE], ones, flat(onehot), start=True, stop=True).then_inc(s_rp, 1)
            for g in range(NC // GT):
                pe.wait_ge(s_ohs, 2 * g + 2)
                pe.wait_ge(s_ohb, 2 * (g + 1))
                for c in range(GT * g, GT * g + GT):
                    mm = pe.matmul(bank[2][:, 0:values * COLS], oh_slot[g % 2][:, c % GT, :], oh_blk[:, :, c, :],
                                   start=(c == 0), stop=(c == NC - 1))
                mm.then_inc(s_inv, 1)

            pe.wait_ge(s_route, 2)
            pe.wait_ge(s_early, 32 * (NE - LATE))
            pe.wait_ge(s_late, 32 * LATE + 32)

            def experts(j):
                return [pe.value_load(eb_i[0:1, bass.ds(4 * j + r, 1)], min_val=0, max_val=NE - 1)
                        for r in range(-1, 3)]

            def bstep(i, r, held):
                ok = lambda k: not isinstance(k, int) or 0 <= k < BLOCKS
                if ok(i + 1):
                    c, q = i + 1, (r + 1) % 4
                    wait(pe, g_x[q], 4 * (c - q) + 16)
                    wait(pe, g_xte, c)
                    for k in range(KD):
                        mm = pe.transpose(bank[0][:, k * P:(k + 1) * P], xg[q][:, k * P:(k + 1) * P], ident)
                    mm.then_inc(g_xt, 1)
                if ok(i):
                    c, p = i, r % 2
                    wait(pe, g_cur, 2 * c + 2)
                    wait(pe, g_xte, c + 1)
                    wait(pe, g_h, 2 * (c - 1))
                    for m in range(KF):
                        for k in range(KD):
                            mm = pe.matmul(bank[(1, 6)[p] + m // 4][:, (m % 4) * P:(m % 4 + 1) * P],
                                           w1_cur[p][:, k, m * P:(m + 1) * P], xgT[p][:, k, :],
                                           start=(k == 0), stop=(k == KD - 1))
                        if m % 4 == 3:
                            mm.then_inc(g_w1, 1)
                if ok(i - 1):
                    c, p = i - 1, (r - 1) % 2
                    wait(pe, g_h, 2 * c + 2)
                    wait(pe, g_r, 4 * (c - 2) + 1)
                    e = held[r] if held is not None else pe.value_load(eb_i[0:1, c:c + 1], min_val=0, max_val=NE - 1)
                    for k in range(KF):
                        mm = pe.matmul(bank[3 + p][:, 0:D], hT[p][:, k, :], w2_sb[:, bass.ds(e, 1), k, :]
                                       .rearrange("p o d -> p (o d)"), start=(k == 0), stop=(k == KF - 1))
                    mm.then_inc(g_w2, 1)

            block_steps(pe, bstep, -1, BLOCKS + 1, experts)

        @block.scalar
        def _(act):
            act.wait_ge(s_param, 48)
            act.activation(negA, negA, ACT.Exp).then_inc(s_negA, 1)

            def dt_out(pair, r):
                act.wait_ge(s_pre_p, pair + 1)
                wait(act, s_pre_dt, pair - 1)
                act.copy(pre_dtT[r % 2][0:NH, :], bank[3 + r % 2][0:NH, 0:NB * P]).then_inc(s_pre_pe, 1)

            def pre_pair(pair, r, part):
                act.wait_ge(s_pre_t, pair + 1)
                wait(act, s_pre_p, pair - 1)
                act.copy(pre_uT[r % 2].rearrange("p k t -> p (k t)"), bank[r % 2][:, :]).then_inc(s_pre_ev, 1)
                if not isinstance(pair, int) or pair > 0:
                    dt_out(pair - 1, (r - 1) % 4)

            def pre_part(part):
                if part == 1:
                    dt_out(NC // NB - 1, 3)
                lo, hi = PARTS[part]
                act.wait_ge(s_sp, 1 + SP_STEPS * part + 2)
                act.activation(dta[:, lo:hi, :], dta[:, lo:hi, :], ACT.Exp, scale=-1.0).then_inc(s_spx, 1)

            pre_steps(act, pre_pair, pre_part)
            act.wait_ge(q_ut, 1)
            act.copy(uT[0].rearrange("p k t -> p (k t)"), bank[0][:, 0:D]).then_inc(q_ute, 1)
            def channels_out(t, par):
                c, p = t, par
                if on(c):
                    wait(act, q_inx, c + 1)
                    wait(act, q_halo, c - 1)
                    for n in range(2):
                        act.copy(xbc[p][:, 3 * n:3 * n + 3, TAPS - 1:], bank[n][:, 0:3 * P]
                                 .rearrange("p (m t) -> p m t", m=3)).then_inc(q_xbe, 1)
                    wait(act, q_silx, c - 1)
                    for m in range(XT_TILES):
                        mm = act.activation(cv[p][:, m, :], bank[m // 3][:, (m % 3) * P:(m % 3 + 1) * P], ACT.Identity,
                                            bias=cb_sb[:, m:m + 1], scale=cw_sb[:, m, TAPS - 1:TAPS])
                    mm.then_inc(q_tap, 1)

            act.wait_ge(s_fill, FILLS)
            channels_out(0, 0)
            act.wait_ge(s_sums, 1)
            flat = lambda v: v.rearrange("p c h -> p (c h)")
            act.activation(flat(e_all), bank[3][:, 0:NC * NH], ACT.Exp).then_inc(s_sumx, 1)
            act.activation(flat(dd_all), bank[4][:, 0:NC * NH], ACT.Exp).then_inc(s_sumx, 1)
            act.activation(flat(cd_all), bank[5][:, 0:NC * NH], ACT.Exp).then_inc(s_sumx, 1)
            act.wait_ge(s_pre, 1)
            act.wait_ge(s_fill, FILLS)

            def transposed(t, par):
                if on(t + 1) or on(t - 5):
                    wait(act, q_ut, t + 2)
                    if on(t - 5):
                        wait(act, q_lg, t - 5)
                        mm = act.copy(x1T.rearrange("p k t -> p (k t)"), bank[0][:, D:2 * D])
                    if on(t + 1):
                        mm = act.copy(uT[1 - par].rearrange("p k t -> p (k t)"), bank[0][:, 0:D])
                    mm.then_inc(q_ute, 1)

            def step(t, par):
                if isinstance(t, int) and t == NC + 3:
                    act.wait_ge(q_yv, 4 * NC)
                    act.wait_ge(q_sq, NC)
                    act.wait_ge(q_s, NC)
                    for e in range(NE - LATE, NE):
                        act.dma_start(w1_sb[:, e, :, :], w1[e].rearrange("(k p) f -> p k f", p=P)).then_inc(s_late, 16)
                        act.dma_start(w2_sb[:, e, :, :], w2[e].rearrange("(k p) d -> p k d", p=P)).then_inc(s_late, 16)
                if isinstance(t, int) and t < NE - LATE:
                    act.dma_start(w1_sb[:, t, :, :], w1[t].rearrange("(k p) f -> p k f", p=P)).then_inc(s_early, 16)
                    act.dma_start(w2_sb[:, t, :, :], w2[t].rearrange("(k p) d -> p k d", p=P)).then_inc(s_early, 16)
                if on(t):
                    wait(act, q_table, t)
                    act.activation(touch, half_neg[:, 0:1], ACT.Exp).then_inc(q_table, 1)
                if not isinstance(t, int) or t > 0:
                    channels_out(t, par)
                early = isinstance(t, int) and t <= 1
                if early:
                    transposed(t, par)
                c, p = t - 1, 1 - par
                if on(c):
                    wait(act, q_seg, c + 1)
                    wait(act, q_y, c - 1)
                    for n in range(2):
                        mm = act.activation(em[p][:, 4 * n:4 * n + 4, :].rearrange("p h l -> p (h l)"), bank[5 + n][:, :],
                                            ACT.Exp)
                    mm.then_inc(q_exp, 1)
                c, p = t - 1, 1 - par
                if on(c):
                    wait(act, q_xt, c + 1)
                    wait(act, q_xdt, c - 1)
                    wait(act, q_xd, c - 1)
                    act.copy(x_sb[p].rearrange("p h d -> p (h d)"), bank[4][:, :]).then_inc(q_xte, 1)
                    wait(act, q_bc, c + 1)
                    wait(act, q_st, c - 1)
                    wait(act, q_cbm, c + 1)
                    act.copy(b_sb[p], bank[7][:, 0:P]).then_inc(q_be, 1)
                c, p = t - 1, 1 - par
                if on(c):
                    wait(act, q_inz, c + 1)
                    wait(act, q_yv, 4 * (c - 1))
                    act.activation(zs[p], bank[2][:, :], ACT.Silu).then_inc(q_silz, 1)
                c, p = t - 3, 1 - par
                if on(c):
                    wait(act, q_yv, 4 * c + 4)
                    wait(act, q_rms, 2 * (c - 1))
                    wait(act, q_sq, c)
                    act.activation(junk, y[p].rearrange("p h d -> p (h d)"), ACT.Square,
                                   accum_out=ssq[:, p:p + 1]).then_inc(q_sq, 1)
                if on(t) and not early:
                    transposed(t, par)
                c, p = t - 3, 1 - par
                if on(c):
                    wait(act, q_yt, c + 1)
                    wait(act, q_op, c)
                    act.copy(yT.rearrange("p k t -> p (k t)"), bank[2][:, :]).then_inc(q_yte, 1)
                if not on(t):
                    transposed(t, par)
                c, p = t, par
                if on(c):
                    wait(act, q_conv, CONV * c + CONV)
                    wait(act, q_y, c - 1)
                    act.activation(xs[p], cv[p], ACT.Silu).then_inc(q_silx, 1)

            mamba_steps(act, step, 0)

            act.wait_ge(s_rv, 2)
            act.activation(ex, lt, ACT.Exp).then_inc(s_rx, 1)
            act.activation(gelu_touch, half_neg[:, 0:1], ACT.Gelu)
            act.wait_ge(s_route, 2)

            def bstep(i, r, held):
                ok = lambda k: not isinstance(k, int) or 0 <= k < BLOCKS
                if ok(i + 1):
                    c, p = i + 1, (r + 1) % 2
                    wait(act, g_xt, c + 1)
                    wait(act, g_w1, 2 * (c - 1))
                    act.copy(xgT[p].rearrange("p k t -> p (k t)"), bank[0][:, 0:D]).then_inc(g_xte, 1)
                if ok(i):
                    c, p = i, r % 2
                    wait(act, g_w2, c - 1)
                    for n in range(2):
                        wait(act, g_w1, 2 * c + n + 1)
                        for m in range(4 * n, 4 * n + 4):
                            mm = act.activation(hT[p][:, m, :], bank[(1, 6)[p] + n][:, (m % 4) * P:(m % 4 + 1) * P],
                                                ACT.Gelu, bias=b1_cur[p][:, m:m + 1])
                        mm.then_inc(g_h, 1)

            block_steps(act, bstep, -1, BLOCKS + 1)

        @block.vector
        def _(dve):
            n = [0]

            def sp_step(ins):
                n[0] += 1
                ins.then_inc(s_sp, 1)
                dve.wait_ge(s_sp, n[0])

            dve.wait_ge(s_negA, 1)
            sp_step(dve.tensor_scalar(negA, negA, -1.0, None, ALU.mult))
            for part, (lo, hi) in enumerate(PARTS):
                psum_dt = bank[(2, 6)[part]][:, lo * NH:hi * NH].rearrange("p (c h) -> p c h", h=NH)
                x, e, d, q, s, dt, a = (v[:, lo:hi, :] for v in (dtx, dta, dts, dtq, dtp, dt_all, a_all))
                row = lambda v: v.unsqueeze(1).broadcast_to([P, hi - lo, NH])
                dve.wait_ge(s_pre_dt, hi // NB)
                sp_step(dve.tensor_tensor(x, psum_dt, row(dtb_row), ALU.add))
                sp_step(dve.scalar_tensor_tensor(out=e, in0=x, scalar=-1.0, in1=x, op0=ALU.mult, op1=ALU.max))
                dve.wait_ge(s_spx, part + 1)
                sp_step(dve.tensor_scalar(d, e, 2.0, None, ALU.add))
                sp_step(dve.reciprocal(d, d))
                sp_step(dve.tensor_tensor(d, d, e, ALU.mult))
                sp_step(dve.tensor_tensor(q, d, d, ALU.mult))
                sp_step(dve.tensor_scalar(s, q, 1.0 / 19, None, ALU.mult))
                for k in range(17, 1, -2):
                    sp_step(dve.scalar_tensor_tensor(out=s, in0=s, scalar=1.0 / k, in1=q, op0=ALU.add, op1=ALU.mult))
                sp_step(dve.scalar_tensor_tensor(out=s, in0=s, scalar=1.0, in1=d, op0=ALU.add, op1=ALU.mult))
                sp_step(dve.tensor_scalar(x, x, 0.0, None, ALU.max))
                sp_step(dve.scalar_tensor_tensor(out=dt, in0=s, scalar=2.0, in1=x, op0=ALU.mult, op1=ALU.add))
                sp_step(dve.tensor_tensor(a, dt, row(negA), ALU.mult))
            assert n[0] == 1 + 2 * SP_STEPS, n[0]
            dve.tensor_scalar(a_hi.bitcast(I32), a_all.bitcast(I32), HI_BITS, None, ALU.bitwise_and).then_inc(s_split, 1)
            dve.wait_ge(s_split, 1)
            dve.tensor_tensor(a_lo, a_all, a_hi, ALU.subtract).then_inc(s_split, 1)
            dve.tensor_copy(mask_gt, masks[:, M_GT, :]).then_inc(s_split, 1)
            dve.wait_ge(s_param2, 112)
            for k in range(KI):
                mm = dve.tensor_scalar(w_out[:, k, :], w_out[:, k, :], nw_col[:, k:k + 1], None, ALU.mult)
            mm.then_inc(s_wout, 1)
            dve.wait_ge(s_sumx, 2)
            dve.tensor_tensor(dd_all, dd_all, dt_all, ALU.mult).then_inc(s_pre, 1)
            dve.wait_ge(s_sumx, 3)
            dve.wait_ge(s_pre, 1)
            dve.wait_ge(s_fill, FILLS)

            def step(t, par):
                def taps(c, p, k):
                    wait(dve, q_conv, CONV * c + XT_TILES * k) if k else wait(dve, q_tap, c + 1)
                    for m in range(XT_TILES):
                        dve.scalar_tensor_tensor(out=cv[p][:, m, :], in0=xbc[p][:, m, k:k + P],
                                                 scalar=cw_sb[:, m, k:k + 1], in1=cv[p][:, m, :], op0=ALU.mult,
                                                 op1=ALU.add).then_inc(q_conv, 1)

                if on(t):
                    taps(t, par, 0)
                c, p = t - 1, 1 - par
                if on(c):
                    wait(dve, q_bc, c + 1)
                    dve.tensor_tensor(cbm[p], bank[7][:, P:2 * P], masks[:, M_LE, :], ALU.mult).then_inc(q_cbm, 1)
                if on(t):
                    for k in range(1, TAPS - 1):
                        taps(t, par, k)
                    wait(dve, q_conv, CONV * t + CONV)
                    dve.tensor_copy(xbc[par][:, :, 0:TAPS - 1], xbc[par][:, :, P:P + TAPS - 1]).then_inc(q_halo, 1)
                c, p = t - 1, 1 - par
                if on(c):
                    wait(dve, q_xte, c + 1)
                    wait(dve, q_y, c - 1)
                    dve.tensor_tensor(xdt[p], x_sb[p], heads(dt_all, c), ALU.mult).then_inc(q_xdt, 1)
                    wait(dve, q_exp, c + 1)
                    wait(dve, q_cbm, c + 1)
                    dve.tensor_tensor(em[p], em[p], cbm[p].unsqueeze(1).broadcast_to([P, NH, P]),
                                      ALU.mult).then_inc(q_m, 1)
                c, r, p = t - 2, t - 4, par
                if on(c):
                    wait(dve, q_y, c + 1)
                    wait(dve, q_yt, c - 1)
                    wait(dve, q_sq, c - 1)
                    dve.tensor_tensor(y[p], bank[6][:, :].rearrange("p (h d) -> p h d", h=NH), heads(e_all, c),
                                      ALU.mult).then_inc(q_yv, 1)
                if on(r):
                    wait(dve, q_op, r + 1)
                    wait(dve, q_lg, r - 1)
                    wait(dve, q_rms, 2 * r + 2)
                    wait(dve, s_ures[p], 8 * (r - p) + 16)
                    dve.scalar_tensor_tensor(out=u_res[p], in0=bank[3][:, 0:D], scalar=rms[:, p:p + 1], in1=u_res[p],
                                             op0=ALU.mult, op1=ALU.add).then_inc(q_r, 1)
                if on(c):
                    wait(dve, q_yv, 4 * c + 1)
                    dve.tensor_tensor(y[p], bank[5][:, :].rearrange("p (h d) -> p h d", h=NH), y[p],
                                      ALU.add).then_inc(q_yv, 1)
                if on(r):
                    wait(dve, q_r, 3 * r + 1)
                    dve.bn_stats(bst[p], u_res[p]).then_inc(q_r, 1)
                if on(c):
                    wait(dve, q_yv, 4 * c + 2)
                    wait(dve, q_xd, c + 1)
                    dve.tensor_tensor(y[p], y[p], xD[p], ALU.add).then_inc(q_yv, 1)
                if on(r):
                    wait(dve, q_r, 3 * r + 2)
                    wait(dve, q_rstd, 2 * (r - 1))
                    settled(dve, s_dve_turns)
                    dve.bn_aggr(mv[p], bst[p]).then_inc(q_r, 1)
                if on(c):
                    wait(dve, q_yv, 4 * c + 3)
                    wait(dve, q_silz, c + 1)
                    dve.tensor_tensor(y[p].rearrange("p h d -> p (h d)"), y[p].rearrange("p h d -> p (h d)"), zs[p],
                                      ALU.mult).then_inc(q_yv, 1)
                    wait(dve, q_st, c + 1)
                    wait(dve, q_sd, c + 1)
                    dve.tensor_tensor(state[p], bank[4][:, :].rearrange("p (h d) -> p h d", h=NH), sdec[p],
                                      ALU.add).then_inc(q_s, 1)
                if on(t - 6):
                    wait(dve, q_lg, t - 5)
                    dve.tensor_copy(logits[:, bass.ds(t - 6, 1), :].rearrange("p o e -> p (o e)"), bank[3][:, D:D + NE]
                                    ).then_inc(q_lge, 1)
                if on(r):
                    wait(dve, q_rstd, 2 * r + 2)
                    dve.tensor_scalar(u_res[p], u_res[p], mv[p][:, 0:1], rstd[:, p:p + 1], ALU.subtract,
                                      ALU.mult).then_inc(q_x1, 1)

            mamba_steps(dve, step, 0)

            dve.wait_ge(q_lge, NC)
            dve.wait_ge(q_x1, NC)
            r = [0]

            def rv(ins):
                r[0] += 1
                ins.then_inc(s_rv, 1)
                dve.wait_ge(s_rv, r[0])

            over_e = lambda v: v.unsqueeze(2).broadcast_to([P, NC, NE])
            mx, sm, prob, ms, pos, slot, blk, prob_hi, prob_lo = (small[:, k, :] for k in range(9))
            tmp_i, slot_i, blk_i = (small[:, k, :].bitcast(I32) for k in range(9, 12))
            rv(dve.tensor_reduce(mx, logits, AX, ALU.max))
            rv(dve.tensor_tensor(lt, logits, over_e(mx), ALU.subtract))
            dve.wait_ge(s_rx, 1)
            rv(dve.tensor_reduce(sm, ex, AX, ALU.add))
            rv(dve.tensor_reduce(mx, ex, AX, ALU.max))
            rv(dve.tensor_tensor(lt, ex, over_e(mx), ALU.is_equal))
            rv(dve.tensor_tensor(lt, lt, prio.unsqueeze(1).broadcast_to([P, NC, NE]), ALU.mult))
            rv(dve.tensor_reduce(ms, lt, AX, ALU.max))
            rv(dve.tensor_tensor(onehot, lt, over_e(ms), ALU.is_equal))
            assert r[0] == ROUTE_ONEHOT
            rv(dve.reciprocal(prob, sm))
            rv(dve.tensor_scalar(prob_hi.bitcast(I32), prob.bitcast(I32), HI_BITS, None, ALU.bitwise_and))
            rv(dve.tensor_tensor(prob_lo, prob, prob_hi, ALU.subtract))
            pad, epad = NC // 2, NE // 2
            for buf in (pref[0][:, 0:pad, :], pref[1][:, 0:pad, :], ends[0][:, 0:epad], ends[1][:, 0:epad]):
                rv(dve.memset(buf, 0.0))
            dve.wait_ge(s_rp, 1)
            totals = bank[1][:, 0:NC * NE].rearrange("p (c e) -> p c e", e=NE)
            rv(dve.tensor_copy(pref[0][:, pad:, :], totals))
            a, d = 0, 1
            while d < NC:
                rv(dve.tensor_tensor(pref[1 - a][:, pad:, :], pref[a][:, pad:, :], pref[a][:, pad - d:pad - d + NC, :],
                                     ALU.add))
                a, d = 1 - a, 2 * d
            upto = pref[a][:, pad:, :]
            blocks_i, start = tiny[:, 0, :], tiny[:, 1, :]
            blocks = tiny[:, 2, :]
            rv(dve.tensor_scalar(blocks, upto[:, NC - 1, :], float(P - 1), None, ALU.add))
            rv(dve.tensor_copy(blocks_i.bitcast(I32), blocks))
            rv(dve.tensor_scalar(blocks_i.bitcast(I32), blocks_i.bitcast(I32), 7, None, ALU.logical_shift_right))
            rv(dve.tensor_copy(ends[0][:, epad:], blocks_i.bitcast(I32)))
            rv(dve.tensor_copy(blocks, ends[0][:, epad:]))
            b, d = 0, 1
            while d < NE:
                rv(dve.tensor_tensor(ends[1 - b][:, epad:], ends[b][:, epad:], ends[b][:, epad - d:epad - d + NE], ALU.add))
                b, d = 1 - b, 2 * d
            end = ends[b][:, epad:]
            rv(dve.tensor_tensor(start, end, blocks, ALU.subtract))
            rv(dve.tensor_scalar(start, start, float(P), None, ALU.mult))
            rv(dve.tensor_tensor(lt, upto, totals, ALU.subtract))
            rv(dve.tensor_tensor(lt, lt, start.unsqueeze(1).broadcast_to([P, NC, NE]), ALU.add))
            rv(dve.tensor_tensor(lt.rearrange("p c e -> p (c e)"), bank[0][:, 0:NC * NE],
                                 lt.rearrange("p c e -> p (c e)"), ALU.add))
            rv(dve.tensor_tensor(lt, lt, onehot, ALU.mult))
            rv(dve.tensor_reduce(pos, lt, AX, ALU.add))
            rv(dve.tensor_copy(tmp_i, pos))
            rv(dve.tensor_scalar(slot_i, tmp_i, P - 1, None, ALU.bitwise_and))
            rv(dve.tensor_scalar(blk_i, tmp_i, 7, None, ALU.logical_shift_right))
            rv(dve.tensor_copy(slot, slot_i))
            rv(dve.tensor_copy(blk, blk_i))
            for par in range(2):
                dve.wait_ge(s_x1st[par], 16 * NC // 2)
            for g in range(NC // GT):
                cs = slice(g * GT, g * GT + GT)
                dve.tensor_tensor(blk_eq[:, cs, :], iota_blk.unsqueeze(1).broadcast_to([P, GT, COLS]),
                                  blk[:, cs].unsqueeze(2).broadcast_to([P, GT, COLS]), ALU.is_equal).then_inc(s_ohe, 1)
                wait(dve, s_inv, g - 1)
                dve.tensor_tensor(oh_slot[g % 2], iota_slot.unsqueeze(1).broadcast_to([P, GT, P]),
                                  slot[:, cs].unsqueeze(2).broadcast_to([P, GT, P]), ALU.is_equal).then_inc(s_ohs, 1)
                dve.wait_ge(s_ohe, g + 1)
                dve.tensor_tensor(oh_blk[:, 2, cs, :], blk_eq[:, cs, :],
                                  prob_lo[:, cs].unsqueeze(2).broadcast_to([P, GT, COLS]), ALU.mult).then_inc(s_ohs, 1)
            rv(dve.tensor_tensor(ge, iota_blk.unsqueeze(2).broadcast_to([P, COLS, NE]),
                                 end.unsqueeze(1).broadcast_to([P, COLS, NE]), ALU.is_ge))
            rv(dve.tensor_reduce(eb_f, ge, AX, ALU.add))
            rv(dve.tensor_scalar(eb_f, eb_f, float(NE - 1), None, ALU.min))
            rv(dve.tensor_copy(eb_i, eb_f))
            dve.wait_ge(s_inv, NC // GT)
            rv(dve.tensor_scalar(idx_z, bank[2][:, 0:COLS], 0.0, float(T + 1), ALU.is_equal, ALU.mult))
            rv(dve.scalar_tensor_tensor(out=idx_f, in0=bank[2][:, 0:COLS], scalar=-1.0, in1=idx_z,
                                        op0=ALU.add, op1=ALU.add))
            dve.tensor_copy(idx_i, idx_f).then_inc(s_route, 1)
            rv(dve.tensor_copy(prob_blk, bank[2][:, COLS:2 * COLS]))
            dve.tensor_tensor(prob_blk, bank[2][:, 2 * COLS:3 * COLS], prob_blk, ALU.add).then_inc(s_route, 1)
            dve.wait_ge(s_route, 2)
            dve.wait_ge(s_early, 32 * (NE - LATE))
            dve.wait_ge(s_late, 32 * LATE + 32)

            def experts(j):
                return [dve.value_load(eb_i[0:1, bass.ds(4 * j + r, 1)], min_val=0, max_val=NE - 1)
                        for r in range(-1, 5)]

            def bstep(i, r, held):
                ok = lambda k: not isinstance(k, int) or 0 <= k < BLOCKS

                def expert(k, n):
                    if held is not None:
                        return held[n + 1]
                    return dve.value_load(eb_i[0:1, k:k + 1], min_val=0, max_val=NE - 1)

                if ok(i + 1):
                    c, p = i + 1, (r + 1) % 2
                    e = expert(c, r + 1)
                    wait(dve, g_w1, 2 * (c - 1))
                    dve.tensor_copy(w1_cur[p].rearrange("p k f -> p (k f)"), w1_sb[:, bass.ds(e, 1), :, :]
                                    .rearrange("p o k f -> p (o k f)")).then_inc(g_cur, 1)
                    wait(dve, g_h, 2 * (c - 1))
                    dve.tensor_copy(b1_cur[p], b1_col[:, bass.ds(e, 1), :].rearrange("p o k -> p (o k)")
                                    ).then_inc(g_cur, 1)
                if ok(i - 1):
                    c, q, p = i - 1, (r - 1) % 4, (r - 1) % 2
                    wait(dve, g_w2, c + 1)
                    wait(dve, g_out[q], 4 * (c - q))
                    e = expert(c, r - 1)
                    dve.tensor_tensor(yo[q], bank[3 + p][:, 0:D], b2_rep[:, bass.ds(e, 1), :].rearrange("p o d -> p (o d)"),
                                      ALU.add).then_inc(g_r, 1)
                    wait(dve, g_r, 4 * c + 1)
                    dve.scalar_tensor_tensor(out=yo[q], in0=yo[q], scalar=prob_blk[:, bass.ds(c, 1)], in1=xg[q],
                                             op0=ALU.mult, op1=ALU.add).then_inc(g_r, 1)
                    wait(dve, g_r, 4 * c + 2)
                    dve.bn_stats(st2[p], yo[q]).then_inc(g_r, 1)
                    wait(dve, g_r, 4 * c + 3)
                    wait(dve, g_rs, 2 * (c - 1))
                    settled(dve, s_dve_turns)
                    dve.bn_aggr(mv2[p], st2[p]).then_inc(g_r, 1)
                if ok(i - 1):
                    c, q, p = i - 1, (r - 1) % 4, (r - 1) % 2
                    wait(dve, g_rs, 2 * c + 2)
                    dve.tensor_scalar(yo[q], yo[q], mv2[p][:, 0:1], rstd2[p][:, 1:2], ALU.subtract,
                                      ALU.mult).then_inc(g_y, 1)

            block_steps(dve, bstep, -1, BLOCKS + 1, experts)


_INS = ["L0_attn_u", "L0_attn_in_proj_w", "L0_attn_conv_weight", "L0_attn_conv_bias", "L0_attn_dt_bias",
        "L0_attn_A_log", "L0_attn_D_param", "L0_attn_norm_weight", "L0_attn_out_proj_w",
        "L0_ffn_Wr", "L0_ffn_W1", "L0_ffn_b1", "L0_ffn_W2", "L0_ffn_b2"]


def kernel(**inputs):
    import concourse.bacc as bacc
    from concourse.bass_utils import run_bass_kernel_spmd as run

    nc = bacc.Bacc("TRN2", target_bir_lowering=False, num_devices=1)
    arrays, args = {}, []
    channels = lambda a: a.reshape(a.shape[0] // P, P, -1).swapaxes(0, 1)
    for name in _INS:
        a = np.asarray(inputs[name])
        if name.endswith("conv_weight"):
            a = channels(a)
        elif name.endswith(("conv_bias", "norm_weight")):
            a = channels(a)[:, :, 0]
        elif name.endswith("ffn_b1"):
            a = channels(a.reshape(-1))[:, :, 0]
        a = np.ascontiguousarray(a)
        arrays[f"in_{name}"] = a
        args.append(nc.dram_tensor(f"in_{name}", a.shape, mybir.dt.from_np(a.dtype), kind="ExternalInput").ap())
    arrays["in_constants"] = constants()
    args.append(nc.dram_tensor("in_constants", (P, CW), F32, kind="ExternalInput").ap())
    out = nc.dram_tensor("out", (T, D), F32, kind="ExternalOutput").ap()
    build(nc, *args, out)
    r = run(nc, [arrays], core_ids=[0])
    return r.results[0]["out"].reshape(NB, L, D)
```
